# Optimizing a Trainium2 kernel written in Bass

```python
import numpy as np
import jax
import jax.numpy as jnp

def _softmax(x, axis=-1):
    return jax.nn.softmax(x, axis=axis)

def _gelu(x):
    return jax.nn.gelu(x, approximate=True)

def _silu(x):
    return jax.nn.silu(x)

def _sigmoid(x):
    return jax.nn.sigmoid(x)

def _layernorm(x, axis=-1, eps=1e-05):
    m = jnp.mean(x, axis=axis, keepdims=True)
    v = jnp.var(x, axis=axis, keepdims=True)
    return (x - m) / jnp.sqrt(v + eps)

def _scatter_add(tgt, idx, src, axis=0):
    return tgt.at[idx].add(src)

def _segment_sum(src, seg, n):
    return jax.ops.segment_sum(src, seg, n)
kernel_name = 'mk_seq_preln_d1_jaxref_r8_9fbb9d'

def setup_inputs(seed: int=0):
    np.random.seed(seed)
    _w = jnp.asarray

    def _L0_attn_setup():
        import jax, jax.numpy as jnp
        import numpy as np
        import math
        EMBED_DIM = 256
        N_HEADS = 16
        HEAD_DIM = EMBED_DIM // N_HEADS
        THETA_BASE = 10000.0

        def _rope_freqs(seq_len):
            i = jnp.arange(HEAD_DIM // 2, dtype=jnp.float32)
            inv_freq = 1.0 / THETA_BASE ** (2.0 * i / HEAD_DIM)
            pos = jnp.arange(seq_len, dtype=jnp.float32)
            th = jnp.outer(pos, inv_freq)
            return (jnp.cos(th), jnp.sin(th))

        def _rope(t, cos, sin):
            b, h, s, d = t.shape
            tr = t.reshape(b, h, s, d // 2, 2)
            x0, x1 = (tr[..., 0], tr[..., 1])
            r0 = x0 * cos - x1 * sin
            r1 = x0 * sin + x1 * cos
            return jnp.stack([r0, r1], axis=-1).reshape(b, h, s, d)
        key = jax.random.key(seed)
        k1, k2, k3 = jax.random.split(key, 3)
        B, S = (2, 256)
        x = jax.random.normal(k1, (B, S, EMBED_DIM), jnp.float32)
        scale = EMBED_DIM ** (-0.5)
        Wqkv = jax.random.normal(k2, (EMBED_DIM, 3 * EMBED_DIM), jnp.float32) * scale
        Wo = jax.random.normal(k3, (EMBED_DIM, EMBED_DIM), jnp.float32) * scale
        return {'x': x, 'Wqkv': Wqkv, 'Wo': Wo}
    _L0_attn_in = _L0_attn_setup()

    def _L0_ffn_setup():
        import jax, jax.numpy as jnp
        import numpy as np
        DIM = 256
        INTER = 176
        E = 16
        TOPK = 4
        G = 4
        TOPK_G = 2
        N_SHARED = 2
        SHARED_INTER = N_SHARED * INTER
        ROUTE_SCALE = 1.0

        def _moe_forward(x, Wg, W1, W3, W2, Ws1, Ws3, Ws2):
            B, S, D = x.shape
            xt = x.reshape(-1, D)
            T = xt.shape[0]
            scores = jax.nn.softmax(xt @ Wg.T, axis=-1)
            sg = scores.reshape(T, G, E // G)
            group_scores = sg.max(axis=-1)
            gidx = jax.lax.top_k(group_scores, TOPK_G)[1]
            gmask = jax.nn.one_hot(gidx, G, dtype=jnp.float32).sum(axis=1) > 0
            masked = jnp.where(gmask[:, :, None], sg, -jnp.inf).reshape(T, E)
            topi = jax.lax.top_k(masked, TOPK)[1]
            weights = jnp.take_along_axis(scores, topi, axis=1) * ROUTE_SCALE
            combine = jnp.zeros((T, E), xt.dtype).at[jnp.arange(T)[:, None], topi].add(weights)
            h = jax.nn.silu(jnp.einsum('td,eid->eti', xt, W1)) * jnp.einsum('td,eid->eti', xt, W3)
            expert_out = jnp.einsum('eti,edi->etd', h, W2)
            y = jnp.einsum('etd,te->td', expert_out, combine)
            z = jax.nn.silu(xt @ Ws1.T) * (xt @ Ws3.T) @ Ws2.T
            return (y + z).reshape(B, S, D)
        key = jax.random.key(seed)
        ks = jax.random.split(key, 8)
        s = 0.02
        x = jax.random.normal(ks[0], (1, 256, DIM), dtype=jnp.float32)
        Wg = jax.random.normal(ks[1], (E, DIM), dtype=jnp.float32) * s
        W1 = jax.random.normal(ks[2], (E, INTER, DIM), dtype=jnp.float32) * s
        W3 = jax.random.normal(ks[3], (E, INTER, DIM), dtype=jnp.float32) * s
        W2 = jax.random.normal(ks[4], (E, DIM, INTER), dtype=jnp.float32) * s
        Ws1 = jax.random.normal(ks[5], (SHARED_INTER, DIM), dtype=jnp.float32) * s
        Ws3 = jax.random.normal(ks[6], (SHARED_INTER, DIM), dtype=jnp.float32) * s
        Ws2 = jax.random.normal(ks[7], (DIM, SHARED_INTER), dtype=jnp.float32) * s
        return {'x': x, 'Wg': Wg, 'W1': W1, 'W3': W3, 'W2': W2, 'Ws1': Ws1, 'Ws3': Ws3, 'Ws2': Ws2}
    _L0_ffn_in = _L0_ffn_setup()
    _d = {'L0_attn_x': _L0_attn_in['x'], 'L0_attn_Wqkv': _L0_attn_in['Wqkv'], 'L0_attn_Wo': _L0_attn_in['Wo'], 'L0_ffn_Wg': _L0_ffn_in['Wg'], 'L0_ffn_W1': _L0_ffn_in['W1'], 'L0_ffn_W3': _L0_ffn_in['W3'], 'L0_ffn_W2': _L0_ffn_in['W2'], 'L0_ffn_Ws1': _L0_ffn_in['Ws1'], 'L0_ffn_Ws3': _L0_ffn_in['Ws3'], 'L0_ffn_Ws2': _L0_ffn_in['Ws2']}
    _x0 = _d['L0_attn_x']
    _d['L0_attn_x'] = jax.random.normal(jax.random.fold_in(jax.random.key(seed), 1), (16, 256, 256), dtype=_x0.dtype)
    del _x0
    return _d

def reference(L0_attn_x, L0_attn_Wqkv, L0_attn_Wo, L0_ffn_Wg, L0_ffn_W1, L0_ffn_W3, L0_ffn_W2, L0_ffn_Ws1, L0_ffn_Ws3, L0_ffn_Ws2):

    def _L0_attn_ref(x, Wqkv, Wo):
        import jax, jax.numpy as jnp
        import numpy as np
        import math
        EMBED_DIM = 256
        N_HEADS = 16
        HEAD_DIM = EMBED_DIM // N_HEADS
        THETA_BASE = 10000.0

        def _rope_freqs(seq_len):
            i = jnp.arange(HEAD_DIM // 2, dtype=jnp.float32)
            inv_freq = 1.0 / THETA_BASE ** (2.0 * i / HEAD_DIM)
            pos = jnp.arange(seq_len, dtype=jnp.float32)
            th = jnp.outer(pos, inv_freq)
            return (jnp.cos(th), jnp.sin(th))

        def _rope(t, cos, sin):
            b, h, s, d = t.shape
            tr = t.reshape(b, h, s, d // 2, 2)
            x0, x1 = (tr[..., 0], tr[..., 1])
            r0 = x0 * cos - x1 * sin
            r1 = x0 * sin + x1 * cos
            return jnp.stack([r0, r1], axis=-1).reshape(b, h, s, d)
        B, S, E = x.shape
        H, D = (N_HEADS, E // N_HEADS)
        qkv = x @ Wqkv
        q, k, v = jnp.split(qkv, 3, axis=-1)
        heads = lambda t: t.reshape(B, S, H, D).transpose(0, 2, 1, 3)
        q, k, v = (heads(q), heads(k), heads(v))
        cos, sin = _rope_freqs(S)
        q = _rope(q, cos, sin)
        k = _rope(k, cos, sin)
        scores = jnp.einsum('bhqd,bhkd->bhqk', q, k) / math.sqrt(D)
        causal = jnp.tril(jnp.ones((S, S), dtype=bool))
        scores = jnp.where(causal, scores, -jnp.inf)
        attn = jax.nn.softmax(scores, axis=-1)
        op = jnp.einsum('bhqk,bhkd->bhqd', attn, v)
        op = op.transpose(0, 2, 1, 3).reshape(B, S, E)
        return op @ Wo

    def _L0_ffn_ref(x, Wg, W1, W3, W2, Ws1, Ws3, Ws2):
        import jax, jax.numpy as jnp
        import numpy as np
        DIM = 256
        INTER = 176
        E = 16
        TOPK = 4
        G = 4
        TOPK_G = 2
        N_SHARED = 2
        SHARED_INTER = N_SHARED * INTER
        ROUTE_SCALE = 1.0

        def _moe_forward(x, Wg, W1, W3, W2, Ws1, Ws3, Ws2):
            B, S, D = x.shape
            xt = x.reshape(-1, D)
            T = xt.shape[0]
            scores = jax.nn.softmax(xt @ Wg.T, axis=-1)
            sg = scores.reshape(T, G, E // G)
            group_scores = sg.max(axis=-1)
            gidx = jax.lax.top_k(group_scores, TOPK_G)[1]
            gmask = jax.nn.one_hot(gidx, G, dtype=jnp.float32).sum(axis=1) > 0
            masked = jnp.where(gmask[:, :, None], sg, -jnp.inf).reshape(T, E)
            topi = jax.lax.top_k(masked, TOPK)[1]
            weights = jnp.take_along_axis(scores, topi, axis=1) * ROUTE_SCALE
            combine = jnp.zeros((T, E), xt.dtype).at[jnp.arange(T)[:, None], topi].add(weights)
            h = jax.nn.silu(jnp.einsum('td,eid->eti', xt, W1)) * jnp.einsum('td,eid->eti', xt, W3)
            expert_out = jnp.einsum('eti,edi->etd', h, W2)
            y = jnp.einsum('etd,te->td', expert_out, combine)
            z = jax.nn.silu(xt @ Ws1.T) * (xt @ Ws3.T) @ Ws2.T
            return (y + z).reshape(B, S, D)
        return _moe_forward(x, Wg, W1, W3, W2, Ws1, Ws3, Ws2)
    x = L0_attn_x
    x = x + _L0_attn_ref(_layernorm(x, axis=-1), L0_attn_Wqkv, L0_attn_Wo)
    x = x + _L0_ffn_ref(_layernorm(x, axis=-1), L0_ffn_Wg, L0_ffn_W1, L0_ffn_W3, L0_ffn_W2, L0_ffn_Ws1, L0_ffn_Ws3, L0_ffn_Ws2)
    return x

_drawn_inputs = setup_inputs


def setup_inputs(seed=0):
    import zlib

    import numpy as np

    out = dict(_drawn_inputs(seed))
    spreads = {}
    factors = {'L0_ffn_Wg': 8.0,
     'L0_ffn_W1': 8.0,
     'L0_ffn_W3': 8.0,
     'L0_ffn_W2': 8.0,
     'L0_ffn_Ws1': 2.945,
     'L0_ffn_Ws3': 2.918,
     'L0_ffn_Ws2': 2.919}
    for name, (base, spread) in spreads.items():
        noise = np.random.default_rng([zlib.crc32(name.encode()), seed]).standard_normal(out[name].shape)
        drawn = base * np.exp(spread * noise) if base else spread * noise
        out[name] = jnp.asarray(drawn.astype(out[name].dtype))
    for name, factor in factors.items():
        out[name] = (out[name] * factor).astype(out[name].dtype)
    return out
```

```python
from contextlib import ExitStack

import concourse.bass as bass
from concourse import mybir

F32 = mybir.dt.float32
F32R = mybir.dt.float32r
BF16 = mybir.dt.bfloat16
I32 = mybir.dt.int32
U32 = mybir.dt.uint32
ALU = mybir.AluOpType
ACT = mybir.ActivationFunctionType
AX = mybir.AxisListType

P = 128
B, S, D = 16, 256, 256
H, HD = 16, 16
PAIRS = HD // 2
TPB = S // P
KT = D // P
T = B * S
NT = T // P
E, TOPK = 16, 4
G, TOPG = 4, 2
I = 176
IC = 88
NC_E = I // IC
SI = 352
NC_S = SI // IC
EPS = 1e-5
VW = 32
SLOT = HD
KB = 3 * SLOT
KA = KB + 2
NEG = -1e30
CAP = T + P
NBLK = T * TOPK // P + E - 1


class Queue:

    def __init__(self, sem):
        self.sem, self.count, self.items = sem, 0, []

    def add(self, build, waits=(), signal=True):
        self.items.append((list(waits), build, self.sem if signal else None, 1))
        if signal:
            self.count += 1
        return (self.sem, self.count)

    def dma(self, build, done, waits=()):
        self.items.append((list(waits), build, done.sem, 16))
        done.count += 16
        return (done.sem, done.count)

    def emit(self, eng):
        reached = {}
        for waits, build, sem, n in self.items:
            for w in waits:
                if w is not None and reached.get(id(w[0]), 0) < w[1]:
                    eng.wait_ge(w[0], w[1])
                    reached[id(w[0])] = w[1]
            ins = build(eng)
            if ins is not None and sem is not None:
                ins.then_inc(sem, n)


class Done:

    def __init__(self, sem):
        self.sem, self.count = sem, 0


def merge(stages):
    live = [[0, n, g] for n, g in stages]
    while live:
        s = min(live, key=lambda v: v[0] / v[1])
        try:
            next(s[2])
            s[0] += 1
        except StopIteration:
            live.remove(s)


def layer_kernel(nc, a, out):
    ctx = ExitStack()
    with ctx:
        part1 = ExitStack()

        def sb(name, shape, dt, scope=None):
            return (scope or ctx).enter_context(nc.sbuf_tensor(name, shape, dt))

        def sb1(name, shape, dt):
            return sb(name, shape, dt, part1)

        def sem(name):
            return ctx.enter_context(nc.semaphore(name))

        def done(name):
            return Done(sem(name))

        pe, act, dve, pool, sp = (Queue(sem(f"s_{n}")) for n in ("pe", "act", "dve", "pool", "sp"))

        qk_scr = nc.dram_tensor("qk_scr", (B, 2, 2, 2, P, S), F32).ap()
        base_scr = nc.dram_tensor("base_scr", (T, D), F32).ap()
        rows_scr = nc.dram_tensor("rows_scr", (E * CAP, D), F32).ap()
        y_scr = nc.dram_tensor("y_scr", (NBLK * P, D), F32).ap()

        bank = [ctx.enter_context(nc.psum_tensor(f"bank{i}", [P, 512], F32)) for i in range(8)]
        free = [[] for _ in range(8)]
        MISC, SCORE_Q, SCORE_K, OUT = [0, 1, 2], [3, 4], [5, 6], [7]
        turn = {id(r): 0 for r in (MISC, SCORE_Q, SCORE_K, OUT)}

        def take(ring):
            i = ring[turn[id(ring)] % len(ring)]
            turn[id(ring)] += 1
            return i

        ident = sb("ident", [P, P], F32)
        idx_all = sb("idx_all", [P, NT, TOPK], I32)
        slot = sb("slot", [P, NT * TOPK], I32)
        w_all = sb("w_all", [P, NT, TOPK], F32)
        e_all = sb("e_all", [P, NT, TOPK], F32)
        chosen = sb("chosen", [P, E], BF16)
        ones_b = sb("ones_b", [P, P], BF16)
        iota_e = sb("iota_e", [P, E], F32)
        region = sb("region", [P, E], F32)
        ident_b = sb1("ident_b", [P, P], BF16)
        mask_b = sb1("mask_b", [P, 2, P], BF16)
        before_b = sb1("before_b", [P, P], BF16)
        half_pow = sb1("half_pow", [P, TPB], F32)
        cos_t, sin_t = sb1("cos_t", [P, S], F32), sb1("sin_t", [P, S], F32)

        def pair(name, shape, scope=part1):
            return [sb(f"{name}_{p}", shape, F32R, scope) for p in ("hi", "lo")]

        wqkv = pair("wqkv", [P, KT, 3 * D])
        wo = pair("wo", [P, KT, D])
        wsg = pair("wsg", [P, KT, 2 * SI + E])
        ws2 = pair("ws2", [IC, NC_S, D])
        wstage = sb1("wstage", [P, 2 * 3 * D], F32)

        NX, NV, NPT = 5, 3, 2
        x_in = [sb1(f"x_in{i}", [P, TPB, D], F32) for i in range(NX)]
        stats = [sb1(f"stats{i}", [P, TPB, 6], F32) for i in range(2)]
        mv = [sb1(f"mv{i}", [P, TPB, 2], F32) for i in range(2)]
        veps = [sb1(f"veps{i}", [P, TPB], F32) for i in range(2)]
        rstd = [sb1(f"rstd{i}", [P, TPB], F32) for i in range(2)]
        xn = sb1("xn", [P, TPB, D], F32)
        xT = pair("xT", [P, KT, S])
        rope_a, rope_b = sb1("rope_a", [P, 2, S], F32), sb1("rope_b", [P, 2, S], F32)
        roped = sb1("roped", [P, 2, 2, S], F32)
        ropeds = pair("ropeds", [P, 2, 2, S])
        qst, kst = sb1("qst", [P, H, S], F32R), sb1("kst", [P, H, S], F32R)
        vhat = [sb1(f"vhat{i}", [P, TPB, H, VW], F32) for i in range(NV)]
        row_max = sb1("row_max", [P, TPB, H], F32)
        nmax = sb1("nmax", [H, 2, S], F32R)
        probs = [sb1(f"probs{i}", [P, 3, 4, P], F32) for i in range(NPT)]
        oT = [sb1(f"oT{i}", [P, 4, S], F32) for i in range(2)]
        rsum = sb1("rsum", [P, TPB, H], F32)
        o_sb = sb1("o_sb", [P, TPB, D], F32)
        oTn = pair("oTn", [P, KT, S])
        x1 = sb1("x1", [P, TPB, D], F32)
        xn2 = [sb1(f"xn2_{i}", [P, TPB, D], F32) for i in range(2)]
        x2T = pair("x2T", [P, KT, S])
        gate_t = sb1("gate_t", [P, SI], F32)
        gate_u = sb1("gate_u", [P, SI], F32)
        hid = sb1("hid", [P, SI], F32)
        hidT = pair("hidT", [IC, NC_S, P])
        base = [sb1(f"base{i}", [P, TPB, D], F32) for i in range(2)]
        lg = sb1("lg", [P, TPB, E], F32)
        lmax = sb1("lmax", [P, TPB], F32)
        lsum = sb1("lsum", [P, TPB], F32)
        score = sb1("score", [P, TPB, E], F32)
        g8 = sb1("g8", [P, TPB, 8], F32)
        gtop = sb1("gtop", [P, TPB, 8], F32)
        gidx = sb1("gidx", [P, TPB, 8], U32)
        gidf = sb1("gidf", [P, TPB, TOPG], F32)
        geq = sb1("geq", [P, TPB, TOPG, G], F32)
        gsel = sb1("gsel", [P, TPB, G], F32)
        masked = sb1("masked", [P, TPB, E], F32)
        etop = sb1("etop", [P, TPB, 8], F32)
        eidx = sb1("eidx", [P, TPB, 8], U32)
        eidf = sb1("eidf", [P, TPB, TOPK], F32)
        onehot = sb1("onehot", [P, TPB, TOPK, E], F32)
        picks = sb1("picks", [P, TPB, E], BF16)
        place = sb1("place", [P, TPB, E], F32)
        placed = sb1("placed", [P, TPB, TOPK, E], F32)

        d_const = done("d_const")
        d_stage = done("d_stage")
        d_x = [done(f"d_x{i}") for i in range(NX)]
        d_scr = done("d_scr")
        d_stack = [done(f"d_stack{i}") for i in range(2)]
        d_nmax = [done(f"d_nmax{i}") for i in range(2)]
        d_base = [done(f"d_base{i}") for i in range(2)]
        d_rows = [done(f"d_rows{i}") for i in range(2)]

        sp.dma(lambda e: e.dma_start(cos_t[:], a["rope_cos"]), d_const)
        c_rope = sp.dma(lambda e: e.dma_start(sin_t[:], a["rope_sin"]), d_const)

        def load_x(b):
            return sp.dma(lambda e: e.dma_start(x_in[b % NX][:], a["x"][b].rearrange("(i p) d -> p i d", p=P)),
                          d_x[b % NX], [x_read.get(b - NX)])

        x_read, x_ready = {}, {}
        x_ready[0] = load_x(0)

        pool.add(lambda e: e.memset(ident[:], 0.0))
        z = pool.add(lambda e: e.memset(half_pow[:], -0.5))
        c_ident = pool.add(lambda e: e.affine_select(out=ident[:], in_=ident[:], compare_op=ALU.not_equal, fill=1.0,
                                                     base=0, pattern=[[-1, P]], channel_multiplier=1), [z])
        c_identb = dve.add(lambda e: e.tensor_copy(ident_b[:], ident[:]), [c_ident])
        pool.add(lambda e: e.memset(mask_b[:], 0.0))
        pool.add(lambda e: e.memset(ones_b[:], 1.0))
        pool.add(lambda e: e.memset(chosen[:], 0.0))
        z = pool.add(lambda e: e.memset(before_b[:], 1.0))
        pool.add(lambda e: e.affine_select(out=mask_b[:], in_=mask_b[:], compare_op=ALU.is_ge, fill=NEG,
                                           base=0, pattern=[[0, 2], [-1, P]], channel_multiplier=1), [z])
        c_masks = pool.add(lambda e: e.affine_select(out=before_b[:], in_=before_b[:], compare_op=ALU.is_gt, fill=0.0,
                                                     base=0, pattern=[[1, P]], channel_multiplier=-1), [z])
        pool.add(lambda e: e.iota(iota_e[:], pattern=[[1, E]], base=0, channel_multiplier=0,
                                  allow_small_or_imprecise_dtypes=True))
        c_iota = pool.add(lambda e: e.iota(region[:], pattern=[[CAP, E]], base=0, channel_multiplier=0,
                                           allow_small_or_imprecise_dtypes=True))
        pool.add(lambda e: e.memset(g8[:], -1.0))
        for v in vhat:
            z = pool.add(lambda e, v=v: e.memset(v[:], 0.0))
        for v in vhat:
            c_vhat = pool.add(lambda e, v=v: e.memset(v[:, :, :, HD:HD + 1], 1.0), [z])
        c_kst = dve.add(lambda e: e.memset(kst[:].bitcast(F32), 1.0))

        def split(dst, src, waits_hi, waits_lo=(), src_free=None):
            hi, lo = dst
            t_hi = act.add(lambda e: e.activation(hi, src, ACT.Copy), waits_hi)
            t_lo = dve.add(lambda e: e.tensor_tensor(lo, src, hi.bitcast(F32), ALU.subtract), [t_hi, *waits_lo])
            return t_hi, t_lo

        stage_free = None
        ready = {}
        for name, dst, src, rows in (("wqkv", wqkv, a["wqkv"], P), ("wo", wo, a["wo"], P), ("wsg", wsg, a["wsg"], P),
                                     ("ws2", ws2, a["ws2"], IC)):
            k, n = dst[0].shape[1], dst[0].shape[2]
            view = wstage[0:rows, 0:k * n].rearrange("p (k n) -> p k n", k=k)
            t = sp.dma(lambda e, view=view, src=src, rows=rows: e.dma_start(view, src.rearrange("(k p) n -> p k n", p=rows)),
                       d_stage, [stage_free])
            ready[name] = stage_free = split((dst[0][:], dst[1][:]), view, [t])[1]
            if name == "wqkv":
                x_ready[1] = load_x(1)
        passes = ((0, 0), (0, 1), (1, 0))

        def product(region, stationary, moving, contraction, waits, first_starts=True):
            n = 3 * contraction
            for j in range(n):
                k, (s, m) = j // 3, passes[j % 3]
                t = pe.add(lambda e, k=k, s=s, m=m, j=j: e.matmul(
                    region, stationary(s, k), moving(m, k), start=(j == 0 and first_starts), stop=(j == n - 1),
                    skip_group_check=True), waits if j == 0 else (), signal=(j == n - 1))
            return t

        def norm(x_tile, x_tok, dst, dst_free, which):
            st, m, v, r = stats[which], mv[which], veps[which], rstd[which]
            for i in range(TPB):
                t = dve.add(lambda e, i=i: e.bn_stats(st[:, i, :], x_tile[:, i, :]), [x_tok])
            for i in range(TPB):
                t2 = dve.add(lambda e, i=i: e.bn_aggr(m[:, i, :], st[:, i, :]), [t])
            t = dve.add(lambda e: e.tensor_scalar(v[:], m[:, :, 1], EPS, None, ALU.add), [t2])
            t = pool.add(lambda e: e.tensor_tensor(r[:], v[:], half_pow[:], ALU.pow), [t])
            for i in range(TPB):
                t2 = dve.add(lambda e, i=i: e.tensor_scalar(dst[:, i, :], x_tile[:, i, :], m[:, i, 0:1], r[:, i:i + 1],
                                                            ALU.subtract, ALU.mult), [t, *dst_free])
            return t2

        def turned(src, src_tok, dst, dst_free, extra=()):
            n = take(MISC)
            for k in range(KT):
                for i in range(TPB):
                    t = pe.add(lambda e, k=k, i=i: e.transpose(
                        bank[n][:, k * S + i * P:k * S + (i + 1) * P], src[:, i, k * P:(k + 1) * P], ident[:]),
                        [src_tok, c_ident, *free[n], *extra], signal=(k == KT - 1 and i == TPB - 1))
            view = bank[n][:, 0:KT * S].rearrange("p (k s) -> p k s", k=KT)
            hi, lo = split((dst[0][:], dst[1][:]), view, [t, *dst_free])
            free[n] = [lo]
            return t, lo

        def exact_sum(e, dst, src):
            with nc.allow_low_precision(reason="sums of whole numbers that the type holds exactly"):
                return e.tensor_reduce(dst, src, AX.X, ALU.add)

        q = {}

        def project(b):
            tok = norm(x_in[b % NX], x_ready[b], xn, [q.get(("xn_read", b - 1))], 0)
            yield
            xn_read, xT_ready = turned(xn, tok, xT, [q.get(("xT_read", b - 1))])
            q["xn_read", b] = xn_read
            yield
            banks = []
            for two in range(2):
                n = take(MISC)
                for qk in range(2):
                    col = (2 * qk + two) * P
                    t = product(bank[n][:, qk * S:(qk + 1) * S],
                                lambda s, k, col=col: wqkv[s][:, k, col:col + P],
                                lambda m, k: xT[m][:, k, :], KT, [xT_ready, ready["wqkv"], *free[n]])
                banks.append((n, t))
            (ne, te), (no, to) = banks
            ev, od = (bank[n][:, 0:2 * S].rearrange("p (q s) -> p q s", q=2) for n in (ne, no))
            cosb = cos_t[:].rearrange("p (o s) -> p o s", o=1).to_broadcast([P, 2, S])
            sinb = sin_t[:].rearrange("p (o s) -> p o s", o=1).to_broadcast([P, 2, S])
            w = [q.get(("roped_read", b - 1))]
            t1 = dve.add(lambda e: e.tensor_tensor(rope_a[:], ev, cosb, ALU.mult), [te, c_rope, q.get(("rope_a", b - 1))])
            t2 = dve.add(lambda e: e.tensor_tensor(rope_b[:], od, sinb, ALU.mult), [to, q.get(("rope_b", b - 1))])
            t3 = pool.add(lambda e: e.tensor_tensor(roped[:, 0, :, :], rope_a[:], rope_b[:], ALU.subtract), [t1, t2, *w])
            t4 = dve.add(lambda e: e.tensor_tensor(roped[:, 1, :, :], ev, sinb, ALU.mult), w)
            free[ne] = [t4]
            t5 = dve.add(lambda e: e.tensor_tensor(rope_b[:], od, cosb, ALU.mult), [t3])
            free[no] = [t5]
            t6 = dve.add(lambda e: e.tensor_tensor(roped[:, 1, :, :], roped[:, 1, :, :], rope_b[:], ALU.add), [t4, t5])
            q["rope_a", b], q["rope_b", b] = t3, t6
            yield
            n = take(MISC)
            for i in range(TPB):
                t = product(bank[n][:, i * D:(i + 1) * D],
                            lambda s, k, i=i: xT[s][:, k, i * P:(i + 1) * P],
                            lambda m, k: wqkv[m][:, k, 2 * D:3 * D], KT, free[n])
            q["xT_read", b] = t
            vw = [t, c_vhat, q.get(("pv", b - NV))]
            vt = act.add(lambda e: e.activation(vhat[b % NV][:, :, :, 0:HD],
                                                bank[n][:, 0:TPB * D].rearrange("p (i h d) -> p i h d", i=TPB, h=H),
                                                ACT.Copy), vw)
            q["v", b] = vt
            free[n] = [vt]
            yield
            hi, lo = split((ropeds[0][:], ropeds[1][:]), roped[:], [t3, t6, q.get(("scr_done", b - 1))],
                           [q.get(("scr_done", b - 1))])
            q["roped_read", b] = lo
            for s, t in ((0, hi), (1, lo)):
                for r in range(2):
                    w = sp.dma(lambda e, s=s, r=r: e.dma_start(qk_scr[b, :, s, r].rearrange("q w t -> w q t"),
                                                              ropeds[s][:, r, :, :].bitcast(F32)), d_scr, [t])
            q["scr_done", b] = w
            o = 64 * (b % 2)
            back = [qk_scr[b, j].rearrange("s r (p h) t -> (s r p) h t", h=H) for j in range(2)]
            ws = [w, q.get(("attended", b - 2)), c_kst]
            sp.dma(lambda e: e.dma_start(qst[o:o + SLOT, :, :].bitcast(F32), back[0][0:SLOT]), d_stack[b % 2], ws)
            sp.dma(lambda e: e.dma_start(qst[o + SLOT:o + KB, :, :].bitcast(F32), back[0]), d_stack[b % 2])
            sp.dma(lambda e: e.dma_start(kst[o:o + 2 * SLOT, :, :].bitcast(F32), back[1]), d_stack[b % 2])
            q["stack", b] = sp.dma(lambda e: e.dma_start(kst[o + 2 * SLOT:o + KB, :, :].bitcast(F32), back[1][0:SLOT]),
                                   d_stack[b % 2])

        def row_maxima(b):
            o = 64 * (b % 2)
            for i in range(TPB):
                for h in range(0, H, 2):
                    n = take(SCORE_Q)
                    view = bank[n][:].rearrange("p (h k) -> p h k", h=2)
                    for j in range(2):
                        pe.add(lambda e, j=j, h=h, i=i, n=n: e.matmul(
                            bank[n][:, j * S:(j + 1) * S], qst[o:o + KB, h + j, i * P:(i + 1) * P],
                            kst[o:o + KB, h + j, :], start=(j == 0), stop=False, skip_group_check=True),
                            [q["stack", b], c_kst, *free[n]] if j == 0 else (), signal=False)
                    t = pe.add(lambda e, i=i, view=view: e.matmul(
                        view[:, :, i * P:(i + 1) * P], ident_b[:], mask_b[:], start=False, stop=True,
                        skip_group_check=True), [c_identb, c_masks])
                    tm = dve.add(lambda e, i=i, h=h, view=view: e.tensor_reduce(
                        row_max[:, i, h:h + 2], view[:, :, 0:(i + 1) * P], AX.X, ALU.max),
                        [t, q.get(("max_turned", b - 1))])
                    free[n] = [tm]
                    yield
            n = take(MISC)
            for i in range(TPB):
                t = pe.add(lambda e, i=i: e.transpose(bank[n][0:H, i * P:(i + 1) * P], row_max[:, i, :], ident[:]),
                           [tm, *free[n]], signal=(i == TPB - 1))
            q["max_turned", b] = t
            w = [t, q.get(("nmax_done", b - 1))]
            hi = act.add(lambda e: e.activation(nmax[:, 0, :], bank[n][0:H, 0:S], ACT.Copy, scale=-1.0), w)
            lo = dve.add(lambda e: e.scalar_tensor_tensor(out=nmax[:, 1, :], in0=bank[n][0:H, 0:S], scalar=-1.0,
                                                          in1=nmax[:, 0, :].bitcast(F32), op0=ALU.mult,
                                                          op1=ALU.subtract), [hi])
            free[n] = [lo]
            for j in range(2):
                t = sp.dma(lambda e, j=j: e.dma_start(qst[o + KB + j:o + KB + j + 1, :, :].bitcast(F32),
                                                      nmax[:, j, :].bitcast(F32)), d_nmax[b % 2], [lo])
            q["nmax_done", b] = t

        def attend(b):
            o = 64 * (b % 2)
            pending = None
            for g in range(H // 4):
                pt = probs[(4 * b + g) % NPT]
                for u in range(2):
                    for kt in range(2):
                        n = take(SCORE_K)
                        view = bank[n][:].rearrange("p (h q) -> p h q", h=2)
                        for j in range(2):
                            h = 4 * g + 2 * u + j
                            t = pe.add(lambda e, j=j, h=h, kt=kt, n=n: e.matmul(
                                bank[n][:, j * S:(j + 1) * S], kst[o:o + KA, h, kt * P:(kt + 1) * P],
                                qst[o:o + KA, h, :], start=(j == 0), stop=(j == 1), skip_group_check=True),
                                [q["nmax_done", b], q["stack", b], *free[n]], signal=(j == 1))
                        dst = (pt[:, 0:3:2, 2 * u:2 * u + 2, :].rearrange("p c h q -> p h c q") if kt == 0
                               else pt[:, 1, 2 * u:2 * u + 2, :])
                        src = (view.rearrange("p h (c q) -> p h c q", c=2) if kt == 0 else view[:, :, P:])
                        te = act.add(lambda e, dst=dst, src=src: e.activation(dst, src, ACT.Exp, scale=0.25),
                                     [t, q.get(("pv_read", 4 * b + g - NPT))])
                        free[n] = [te]
                    yield
                diag = pt[:, 0:2, :, :].rearrange("p c h q -> p (c h q)")
                ts = pool.add(lambda e, diag=diag: e.affine_select(
                    out=diag, in_=diag, compare_op=ALU.is_ge, fill=0.0, base=0,
                    pattern=[[0, 8], [1, P]], channel_multiplier=-1), [te])
                if pending:
                    pending()
                    yield

                def weigh(g=g, pt=pt, ts=ts):
                    n = take(OUT)
                    for kt in range(2):
                        for j in range(4):
                            mov = pt[:, 0:3:2, j, :] if kt == 0 else pt[:, 1, j, :]
                            t = pe.add(lambda e, j=j, kt=kt, mov=mov: e.matmul(
                                bank[n][32 * j:32 * j + VW, kt * P:S], vhat[b % NV][:, kt, 4 * g + j, :], mov,
                                start=(kt == 0), stop=(kt == 1), skip_group_check=True),
                                [ts, q["v", b], *free[n]], signal=(kt == 1 and j == 3))
                    q["pv_read", 4 * b + g] = t
                    q["pv", b] = t
                    tc = act.add(lambda e: e.activation(oT[b % 2][:, g, :], bank[n][:, 0:S], ACT.Copy),
                                 [t, q.get(("oT_read", b - 2))])
                    free[n] = [tc]
                    q["oT", b] = tc
                pending = weigh
            q["attended", b] = t
            pending()

        def mix(b):
            for i in range(TPB):
                n = take(MISC)
                for g in range(4):
                    t = pe.add(lambda e, g=g, i=i, n=n: e.transpose(
                        bank[n][:, g * P:(g + 1) * P], oT[b % 2][:, g, i * P:(i + 1) * P], ident[:]),
                        [q["oT", b], *free[n]], signal=(g == 3))
                heads = bank[n][:].rearrange("p (h w) -> p h w", w=VW)
                tr = dve.add(lambda e, i=i, heads=heads: e.reciprocal(rsum[:, i, :], heads[:, :, HD]), [t])
                to = dve.add(lambda e, i=i, heads=heads: e.tensor_tensor(
                    o_sb[:, i, :].rearrange("p (h d) -> p h d", h=H), heads[:, :, 0:HD],
                    rsum[:, i, :].rearrange("p (h o) -> p h o", o=1).to_broadcast([P, H, HD]), ALU.mult),
                    [tr, q.get(("o_read", b - 1))])
                free[n] = [to]
                yield
            q["oT_read", b] = t
            o_read, oTn_ready = turned(o_sb, to, oTn, [q.get(("oTn_read", b - 1))])
            q["o_read", b] = o_read
            yield
            n = take(MISC)
            for i in range(TPB):
                t = product(bank[n][:, i * D:(i + 1) * D], lambda s, k, i=i: oTn[s][:, k, i * P:(i + 1) * P],
                            lambda m, k: wo[m][:, k, :], KT, [oTn_ready, ready["wo"], *free[n]])
            q["oTn_read", b] = t
            t1 = dve.add(lambda e, n=n: e.tensor_tensor(x1[:].rearrange("p i d -> p (i d)"), bank[n][:, 0:TPB * D],
                                                   x_in[b % NX][:].rearrange("p i d -> p (i d)"), ALU.add),
                         [t, q.get(("x1_read", b - 1))])
            free[n] = [t1]
            x_read[b] = t1
            yield
            x2 = xn2[b % 2]
            tn = norm(x1, t1, x2, [q.get(("rows_done", b - 2)), q.get(("x2_turned", b - 2))], 1)
            yield
            x2_turned, x2T_ready = turned(x2, tn, x2T, [q.get(("x2T_read", b - 1))])
            q["x2_turned", b] = x2_turned
            yield
            for i in range(TPB):
                na, nb = take(MISC), take(MISC)
                st = lambda s, k, i=i: x2T[s][:, k, i * P:(i + 1) * P]
                ta = product(bank[na][:, 0:SI + E], st, lambda m, k: wsg[m][:, k, 0:SI + E], KT,
                             [x2T_ready, ready["wsg"], *free[na]])
                tb = product(bank[nb][:, 0:SI], st, lambda m, k: wsg[m][:, k, SI + E:], KT, free[nb])
                tt = act.add(lambda e, na=na: e.activation(gate_t[:], bank[na][:, 0:SI], ACT.Tanh, scale=0.5),
                             [ta, q.get("gate_read")])
                tl = act.add(lambda e, na=na, i=i: e.activation(lg[:, i, :], bank[na][:, SI:SI + E], ACT.Copy),
                             [q.get(("lg_read", b - 1))])
                tu = dve.add(lambda e, na=na: e.scalar_tensor_tensor(out=gate_u[:], in0=gate_t[:], scalar=1.0,
                                                                     in1=bank[na][:, 0:SI], op0=ALU.add,
                                                                     op1=ALU.mult), [tt, tl])
                q["gate_read"] = tu
                free[na] = [tu, tl]
                th = dve.add(lambda e, nb=nb: e.scalar_tensor_tensor(out=hid[:], in0=gate_u[:], scalar=0.5,
                                                                     in1=bank[nb][:, 0:SI], op0=ALU.mult,
                                                                     op1=ALU.mult), [tb, tu, q.get("hid_read")])
                free[nb] = [th]
                yield
                n = take(MISC)
                for c in range(NC_S):
                    t = pe.add(lambda e, c=c, n=n: e.transpose(bank[n][0:IC, c * P:(c + 1) * P],
                                                               hid[:, c * IC:(c + 1) * IC], ident[:]),
                               [th, *free[n]], signal=(c == NC_S - 1))
                q["hid_read"] = t
                hi, lo = split((hidT[0][:], hidT[1][:]), bank[n][0:IC, :].rearrange("p (c t) -> p c t", c=NC_S),
                               [t, q.get("hidT_read")])
                free[n] = [lo]
                yield
                n = take(MISC)
                t = product(bank[n][:, 0:D], lambda s, k: hidT[s][:, k, :], lambda m, k: ws2[m][:, k, :], NC_S,
                            [lo, ready["ws2"], *free[n]])
                q["hidT_read"] = t
                tbase = dve.add(lambda e, n=n, i=i: e.tensor_tensor(base[b % 2][:, i, :], bank[n][:, 0:D], x1[:, i, :],
                                                                   ALU.add), [t, q.get(("base_done", b - 2))])
                free[n] = [tbase]
                yield
            q["x2T_read", b] = tb
            q["x1_read", b] = tbase
            q["base_done", b] = sp.dma(lambda e: e.dma_start(
                base_scr[b * S:(b + 1) * S].rearrange("(i p) d -> p i d", p=P), base[b % 2][:]), d_base[b % 2], [tbase])
            yield from route(b, tl)

        def route(b, tl):
            def v(build, *waits):
                return dve.add(build, waits)

            def bc(ap, shape):
                return ap.to_broadcast(shape)
            t = v(lambda e: e.tensor_reduce(lmax[:], lg[:], AX.X, ALU.max), tl)
            t = v(lambda e: e.tensor_tensor(lg[:], lg[:], bc(lmax[:].rearrange("p (i o) -> p i o", o=1), [P, TPB, E]),
                                            ALU.subtract), t)
            t = act.add(lambda e: e.activation(lg[:], lg[:], ACT.Exp), [t])
            t = v(lambda e: e.tensor_reduce(lsum[:], lg[:], AX.X, ALU.add), t)
            t = v(lambda e: e.reciprocal(lsum[:], lsum[:]), t)
            t = v(lambda e: e.tensor_tensor(score[:], lg[:], bc(lsum[:].rearrange("p (i o) -> p i o", o=1),
                                                               [P, TPB, E]), ALU.mult), t)
            q["lg_read", b] = t
            yield
            by_group = score[:].rearrange("p i (g m) -> p i g m", g=G)
            t = v(lambda e: e.tensor_reduce(g8[:, :, 0:G], by_group, AX.X, ALU.max), t, c_iota)
            for i in range(TPB):
                t2 = v(lambda e, i=i: e.max(gtop[:, i, :], g8[:, i, :]), t)
            for i in range(TPB):
                t = v(lambda e, i=i: e.max_index(gidx[:, i, :], gtop[:, i, :], g8[:, i, :]), t2)
            t = v(lambda e: e.tensor_copy(gidf[:], gidx[:, :, 0:TOPG]), t)
            full = [P, TPB, TOPG, G]
            t = v(lambda e: e.tensor_tensor(
                geq[:], bc(iota_e[:, 0:G].rearrange("p (i k g) -> p i k g", i=1, k=1), full),
                bc(gidf[:].rearrange("p i (k o) -> p i k o", o=1), full), ALU.is_equal), t)
            t = v(lambda e: e.tensor_tensor(gsel[:], geq[:, :, 0, :], geq[:, :, 1, :], ALU.add), t)
            selb = bc(gsel[:].rearrange("p i (g o) -> p i g o", o=1), [P, TPB, G, E // G])
            mview = masked[:].rearrange("p i (g m) -> p i g m", g=G)
            t = v(lambda e: e.tensor_tensor(mview, by_group, selb, ALU.mult), t)
            t = v(lambda e: e.scalar_tensor_tensor(out=mview, in0=selb, scalar=-1.0, in1=mview, op0=ALU.add,
                                                   op1=ALU.add), t)
            yield
            for i in range(TPB):
                t2 = v(lambda e, i=i: e.max(etop[:, i, :], masked[:, i, :]), t)
            for i in range(TPB):
                t = v(lambda e, i=i: e.max_index(eidx[:, i, :], etop[:, i, :], masked[:, i, :]), t2)
            t0 = TPB * b
            v(lambda e: e.tensor_copy(w_all[:, t0:t0 + TPB, :], etop[:, :, 0:TOPK]), t2)
            v(lambda e: e.tensor_copy(e_all[:, t0:t0 + TPB, :], eidx[:, :, 0:TOPK]), t)
            t = v(lambda e: e.tensor_copy(eidf[:], eidx[:, :, 0:TOPK]))
            full2 = [P, TPB, TOPK, E]
            t = v(lambda e: e.tensor_tensor(
                onehot[:], bc(iota_e[:].rearrange("p (i k e) -> p i k e", i=1, k=1), full2),
                bc(eidf[:].rearrange("p i (k o) -> p i k o", o=1), full2), ALU.is_equal), t)
            t = v(lambda e: exact_sum(e, picks[:], onehot.rearrange("p i k e -> p i e k")), t,
                  q.get(("ranked", b - 1)), q.get(("chosen", b - 1)))
            n = take(MISC)
            pe.add(lambda e: e.matmul(bank[n][:, 0:E], before_b[:], picks[:, 0, :], start=True, stop=False,
                                      skip_group_check=True), [t, q.get(("chosen", b - 1)), c_masks, *free[n]], signal=False)
            pe.add(lambda e: e.matmul(bank[n][:, 0:E], ones_b[:], chosen[:], start=False, stop=True,
                                      skip_group_check=True), (), signal=False)
            pe.add(lambda e: e.matmul(bank[n][:, E:2 * E], before_b[:], picks[:, 1, :], start=False, stop=False,
                                      skip_group_check=True), (), signal=False)
            pe.add(lambda e: e.matmul(bank[n][:, E:2 * E], ones_b[:], picks[:, 0, :], start=False, stop=False,
                                      skip_group_check=True), (), signal=False)
            t2 = pe.add(lambda e: e.matmul(bank[n][:, E:2 * E], ones_b[:], chosen[:], start=False, stop=True,
                                           skip_group_check=True))
            q["ranked", b] = t2
            t3 = pool.add(lambda e: e.tensor_tensor(chosen[:], chosen[:], picks[:, 0, :], ALU.add), [t2])
            q["chosen", b] = pool.add(lambda e: e.tensor_tensor(chosen[:], chosen[:], picks[:, 1, :], ALU.add), [t3])
            t = v(lambda e: e.tensor_tensor(place[:], bank[n][:, 0:TPB * E].rearrange("p (i e) -> p i e", i=TPB),
                                            bc(region[:].rearrange("p (i e) -> p i e", i=1), [P, TPB, E]), ALU.add), t2)
            free[n] = [t]
            t = v(lambda e: e.tensor_tensor(placed[:], onehot[:], bc(place[:].rearrange("p i (k e) -> p i k e", k=1),
                                                                     full2), ALU.mult), t)
            t = v(lambda e: exact_sum(e, idx_all[:, t0:t0 + TPB, :], placed[:]), t)
            yield
            for i in range(TPB):
                for k in range(TOPK):
                    w = pool.dma(lambda e, i=i, k=k: e.indirect_dma_start(
                        rows_scr[:, :], bass.IndirectOffsetOnAxis(ap=idx_all[:, t0 + i, k:k + 1].bitcast(U32), axis=0),
                        xn2[b % 2][:, i, :], None), d_rows[b % 2], [t])
            q["rows_done", b] = w

        part1.close()
        LAST = B if not DEBUG_B else DEBUG_B
        for s in range(LAST + 3):
            stages = []
            if 0 <= s - 2 < LAST:
                stages.append((13, attend(s - 2)))
            if 0 <= s - 1 < LAST:
                stages.append((17, row_maxima(s - 1)))
            if s < LAST:
                stages.append((5, project(s)))
            if 0 <= s - 3 < LAST:
                stages.append((15, mix(s - 3)))
            merge(stages)
            if s + 2 < LAST:
                x_ready[s + 2] = load_x(s + 2)

        over = [(u.sem, u.count) for u in (pe, act, dve, pool)]
        over += [(u.sem, u.count) for u in (d_const, d_stage, d_scr, *d_x, *d_stack, *d_nmax, *d_base, *d_rows)]
        part2 = ExitStack()

        def sb2(name, shape, dt):
            return sb(name, shape, dt, part2)

        NXB, NYB, NST = 4, 3, 2
        w13 = pair("w13", [P, E * KT * SI], part2)
        w2 = pair("w2", [IC, E * NC_E * D], part2)
        st13 = [sb2(f"st13_{i}", [P, KT * SI], F32) for i in range(NST)]
        st2 = [sb2(f"st2_{i}", [IC, NC_E * D], F32) for i in range(NST)]
        zero = sb2("zero", [P, D], F32)
        xb = [sb2(f"xb{i}", [P, D], F32) for i in range(NXB)]
        xbT = [pair(f"xbT{i}", [P, KT, P], part2) for i in range(2)]
        silu = sb2("silu", [P, I], F32)
        up = [sb2(f"up{i}", [P, I], F32) for i in range(2)]
        upT = [pair(f"upT{i}", [IC, NC_E, P], part2) for i in range(2)]
        yb = [sb2(f"yb{i}", [P, D], F32) for i in range(NYB)]
        cnt = sb2("cnt", [P, E], F32)
        tail = sb2("tail", [P, E], I32)
        tail_f = sb2("tail_f", [P, E], F32)
        lane = sb2("lane", [P, E], F32)
        nblk_i = sb2("nblk_i", [P, E], I32)
        nblk = sb2("nblk", [P, E], F32)
        zrow = sb2("zrow", [P, E], F32)
        ends = sb2("ends", [P, E], F32)
        shift = sb2("shift", [P, E], F32)
        wide = sb2("wide", [P, NBLK * E], F32)
        shifts = sb2("shifts", [P, NT * TOPK], F32)
        blk = sb2("blk", [1, NBLK], F32)
        wrap = sb2("wrap", [1, NBLK], F32)
        before = sb2("before", [1, NBLK], F32)
        expert = sb2("expert", [1, NBLK], F32)
        row_f = sb2("row_f", [1, NBLK], F32)
        row_t = sb2("row_t", [1, NBLK], I32)
        off13 = sb2("off13", [1, NBLK], I32)
        off2 = sb2("off2", [1, NBLK], I32)
        NG = 4
        d_zero = done("d_zero")
        d_w13 = [done(f"d_w13_{i}") for i in range(NST)]
        d_w2 = [done(f"d_w2_{i}") for i in range(NST)]
        d_xb = [done(f"d_xb{i}") for i in range(NXB)]
        d_yb = [done(f"d_yb{i}") for i in range(NYB)]
        d_gat = [done(f"d_gat{i}") for i in range(NG)]
        d_acc = [done(f"d_acc{i}") for i in range(NG)]
        d_out = [done(f"d_out{i}") for i in range(NG)]

        n = take(MISC)
        tc = pe.add(lambda e: e.matmul(bank[n][:, 0:E], ones_b[:], chosen[:], start=True, stop=True),
                    [q["chosen", LAST - 1], *free[n]])
        tz = pool.add(lambda e: e.memset(zero[:], 0.0), over)
        pool.add(lambda e: e.memset(zrow[:], 0.0))
        pool.add(lambda e: e.iota(blk[:], pattern=[[1, NBLK]], base=0, channel_multiplier=0,
                                  allow_small_or_imprecise_dtypes=True))
        tl = pool.add(lambda e: e.iota(lane[:], pattern=[[CAP, E]], base=0, channel_multiplier=1,
                                       allow_small_or_imprecise_dtypes=True))

        def v(build, *waits):
            return dve.add(build, waits)

        t = v(lambda e: e.tensor_copy(cnt[:], bank[n][:, 0:E]), tc, *over)
        free[n] = [t]
        t2 = v(lambda e: e.tensor_tensor(tail[:], cnt[:], lane[:], ALU.add), t, tl)
        for x in range(E):
            w_zero = pool.dma(lambda e, x=x: e.indirect_dma_start(
                rows_scr[:, :], bass.IndirectOffsetOnAxis(ap=tail[:, x:x + 1].bitcast(U32), axis=0), zero[:], None),
                d_zero, [t2, tz])
        t = v(lambda e: e.tensor_scalar(nblk_i[:], cnt[:], P / 2 - 0.5, 1.0 / P, ALU.add, ALU.mult), t2)
        t = v(lambda e: e.tensor_copy(nblk[:], nblk_i[:]), t)
        t = v(lambda e: e.tensor_tensor_scan(ends[:], nblk[:], zrow[:], 0.0, ALU.add, ALU.add), t)
        t = v(lambda e: e.tensor_scalar(wrap[:], blk[:], ends[0:1, E - 1:E], ends[0:1, E - 1:E], ALU.is_ge, ALU.mult), t)
        t = v(lambda e: e.tensor_tensor(blk[:], blk[:], wrap[:], ALU.subtract), t)
        past = wide[0:1, :].rearrange("p (b e) -> p b e", e=E)
        blke = blk[:].rearrange("p (b o) -> p b o", o=1).to_broadcast([1, NBLK, E])

        def per_e(ap):
            return ap.rearrange("p (o e) -> p o e", o=1).to_broadcast([1, NBLK, E])
        t = v(lambda e: e.tensor_tensor(past, blke, per_e(ends[0:1, :]), ALU.is_ge), t)
        t = v(lambda e: e.tensor_reduce(expert[:], past, AX.X, ALU.add), t)
        t = v(lambda e: e.tensor_tensor(past, past, per_e(nblk[0:1, :]), ALU.mult), t)
        t = v(lambda e: e.tensor_reduce(before[:], past, AX.X, ALU.add), t)
        t = v(lambda e: e.tensor_tensor(row_f[:], blk[:], before[:], ALU.subtract), t)
        t = v(lambda e: e.tensor_scalar(row_f[:], row_f[:], float(P), None, ALU.mult), t)
        t_row = v(lambda e: e.scalar_tensor_tensor(out=row_t[:], in0=expert[:], scalar=float(CAP), in1=row_f[:],
                                                   op0=ALU.mult, op1=ALU.add), t)
        v(lambda e: e.tensor_scalar(off13[:], expert[:], float(KT * SI), None, ALU.mult))
        t_off = v(lambda e: e.tensor_scalar(off2[:], expert[:], float(NC_E * D), None, ALU.mult))

        t = v(lambda e: e.tensor_tensor(shift[:], ends[:], nblk[:], ALU.subtract), t_off)
        t = v(lambda e: e.scalar_tensor_tensor(out=shift[:], in0=shift[:], scalar=float(P), in1=region[:],
                                               op0=ALU.mult, op1=ALU.subtract), t)
        hot = wide[:, 0:NT * TOPK * E].rearrange("p (c e) -> p c e", e=E)
        every = [P, NT * TOPK, E]

        def by_e(ap):
            return ap.rearrange("p (o e) -> p o e", o=1).to_broadcast(every)
        t = v(lambda e: e.tensor_tensor(hot, by_e(iota_e[:]),
                                        e_all[:].rearrange("p t (k o) -> p (t k) o", o=1).to_broadcast(every),
                                        ALU.is_equal), t)
        t = v(lambda e: e.tensor_tensor(hot, hot, by_e(shift[:]), ALU.mult), t)
        t = v(lambda e: e.tensor_reduce(shifts[:], hot, AX.X, ALU.add), t)
        t_slot = v(lambda e: e.tensor_tensor(slot[:], shifts[:], idx_all[:].rearrange("p t k -> p (t k)"), ALU.add), t)

        free13, free2 = [None] * NST, [None] * NST
        for x in range(E):
            i = x % NST
            t = sp.dma(lambda e, x=x, i=i: e.dma_start(st13[i][:].rearrange("p (k n) -> p k n", k=KT),
                                                       a["w13"][x].rearrange("(k p) n -> p k n", p=P)),
                       d_w13[i], [free13[i], *over])
            free13[i] = split([w[:, x * KT * SI:(x + 1) * KT * SI] for w in w13], st13[i][:], [t])[1]
            t = sp.dma(lambda e, x=x, i=i: e.dma_start(st2[i][:].rearrange("p (k n) -> p k n", k=NC_E),
                                                       a["w2"][x].rearrange("(k p) n -> p k n", p=IC)),
                       d_w2[i], [free2[i]])
            free2[i] = split([w[:, x * NC_E * D:(x + 1) * NC_E * D] for w in w2], st2[i][:], [t])[1]
        weights_ready = [free2[(E - 1) % NST]]

        r = {}
        regs = {}

        def fetch(queue, key, table, top, step, waits=()):
            def build(e):
                regs[key] = e.value_load(table, min_val=0, max_val=top)
            queue.add(build, waits, signal=False)

        def load_rows(j):
            fetch(sp, ("x", j), row_t[0:1, j:j + 1], E * CAP - P, P, [t_row])
            r["x", j] = sp.dma(lambda e: e.dma_start(xb[j % NXB][:], rows_scr[bass.ds(regs["x", j], P), :]),
                               d_xb[j % NXB], [w_zero, *((d.sem, d.count) for d in d_rows), r.get(("x_read", j - NXB))])

        def turn_rows(j):
            n = (0, 1)[j % 2]
            for k in range(KT):
                t = pe.add(lambda e, k=k: e.transpose(bank[n][:, k * P:(k + 1) * P], xb[j % NXB][:, k * P:(k + 1) * P],
                                                      ident[:]), [r["x", j], *free[n]], signal=(k == KT - 1))
            r["x_read", j] = t
            hi, lo = split([u[:] for u in xbT[j % 2]], bank[n][:, 0:KT * P].rearrange("p (k t) -> p k t", k=KT),
                           [t, r.get(("xT_read", j - 2))])
            free[n] = [lo]
            r["xT", j] = lo

        def hidden(j):
            n = (2, 3)[j % 2]
            fetch(pe, ("w13", j), off13[0:1, j:j + 1], (E - 1) * KT * SI, SI, [t_off, *weights_ready])
            t = product(bank[n][:, 0:SI], lambda s, k: xbT[j % 2][s][:, k, :],
                        lambda m, k: w13[m][:, bass.ds(regs["w13", j] + k * SI, SI)], KT, [r["xT", j], *free[n]])
            r["xT_read", j] = t
            t = act.add(lambda e: e.activation(silu[:], bank[n][:, 0:I], ACT.Silu), [t, r.get("silu_read")])
            t = dve.add(lambda e: e.tensor_tensor(up[j % 2][:], silu[:], bank[n][:, I:SI], ALU.mult),
                        [t, r.get(("up_read", j - 2))])
            r["silu_read"] = r["up", j] = t
            free[n] = [t]

        def turn_hidden(j):
            n = (4, 5)[j % 2]
            for c in range(NC_E):
                t = pe.add(lambda e, c=c: e.transpose(bank[n][0:IC, c * P:(c + 1) * P],
                                                      up[j % 2][:, c * IC:(c + 1) * IC], ident[:]),
                           [r["up", j], *free[n]], signal=(c == NC_E - 1))
            r["up_read", j] = t
            hi, lo = split([u[:] for u in upT[j % 2]], bank[n][0:IC, 0:NC_E * P].rearrange("p (c t) -> p c t", c=NC_E),
                           [t, r.get(("upT_read", j - 2))])
            free[n] = [lo]
            r["upT", j] = lo

        def result(j):
            n = (6, 7)[j % 2]
            fetch(pe, ("w2", j), off2[0:1, j:j + 1], (E - 1) * NC_E * D, D)
            t = product(bank[n][:, 0:D], lambda s, k: upT[j % 2][s][:, k, :],
                        lambda m, k: w2[m][:, bass.ds(regs["w2", j] + k * D, D)], NC_E, [r["upT", j], *free[n]])
            r["upT_read", j] = t
            t = act.add(lambda e: e.activation(yb[j % NYB][:], bank[n][:, 0:D], ACT.Copy), [t, r.get(("y", j - NYB))])
            free[n] = [t]
            r["y", j] = sp.dma(lambda e: e.dma_start(y_scr[j * P:(j + 1) * P, :], yb[j % NYB][:]),
                               d_yb[j % NYB], [t])

        for j in range(NXB - 1):
            load_rows(j)
        for s in range(NBLK + 3):
            if s < NBLK:
                turn_rows(s)
            if s + NXB - 1 < NBLK:
                load_rows(s + NXB - 1)
            if 0 <= s - 1 < NBLK:
                hidden(s - 1)
            if 0 <= s - 2 < NBLK:
                turn_hidden(s - 2)
            if 0 <= s - 3 < NBLK:
                result(s - 3)

        part2.close()
        part3 = ExitStack()
        gat = [[sb(f"gat{i}_{k}", [P, D], F32, part3) for k in range(TOPK)] for i in range(NG)]
        acc = [sb(f"acc{i}", [P, D], F32, part3) for i in range(NG)]
        y_done = [(d.sem, d.count) for d in d_yb] + [(u.sem, u.count) for u in (pe, act, dve)]
        out_rows = out.rearrange("b s d -> (b s) d")
        for t_ in range(TPB * LAST):
            i = t_ % NG
            rows = slice(t_ * P, (t_ + 1) * P)
            tb = sp.dma(lambda e, i=i, rows=rows: e.dma_start(acc[i][:], base_scr[rows, :]), d_acc[i],
                        [r.get(("out", t_ - NG)), *y_done, *((d.sem, d.count) for d in d_base)])
            for k in range(TOPK):
                tg = pool.dma(lambda e, i=i, k=k, t_=t_: e.indirect_dma_start(
                    gat[i][k][:], None, y_scr[:, :],
                    bass.IndirectOffsetOnAxis(ap=slot[:, t_ * TOPK + k:t_ * TOPK + k + 1].bitcast(U32), axis=0)),
                    d_gat[i], [*y_done, t_slot, r.get(("acc", t_ - NG))])
            t = tb
            for k in range(TOPK):
                t = dve.add(lambda e, i=i, k=k, t_=t_: e.scalar_tensor_tensor(
                    out=acc[i][:], in0=gat[i][k][:], scalar=w_all[:, t_, k:k + 1], in1=acc[i][:], op0=ALU.mult,
                    op1=ALU.add), [tb, tg, t])
            r["acc", t_] = t
            r["out", t_] = sp.dma(lambda e, i=i, rows=rows: e.dma_start(out_rows[rows, :], acc[i][:]), d_out[i], [t])
        part3.close()

        finish(nc, ctx, (sp, act, dve, pool, pe), [d_scr, *d_base, *d_rows, d_zero, *d_yb, *d_out])


DEBUG_B = 0


def finish(nc, ctx, queues, dones):
    sp, act, dve, pool, pe = queues
    with nc.Block() as block:
        @block.sync
        def _(eng):
            sp.emit(eng)
            for d in dones:
                if d.count:
                    eng.wait_ge(d.sem, d.count)

        @block.scalar
        def _(eng):
            act.emit(eng)

        @block.vector
        def _(eng):
            dve.emit(eng)

        @block.gpsimd
        def _(eng):
            pool.emit(eng)

        @block.tensor
        def _(eng):
            pe.emit(eng)


def kernel(L0_attn_x, L0_attn_Wqkv, L0_attn_Wo, L0_ffn_Wg, L0_ffn_W1, L0_ffn_W3, L0_ffn_W2, L0_ffn_Ws1, L0_ffn_Ws3,
           L0_ffn_Ws2):
    import numpy as np
    import concourse.bacc as bacc
    from concourse.bass_utils import run_bass_kernel_spmd

    inv = (1.0 / 10000.0 ** (2.0 * np.arange(PAIRS, dtype=np.float32) / HD)).astype(np.float32)
    angle = np.repeat(np.outer(inv, np.arange(S, dtype=np.float32)).astype(np.float32), H, axis=0)
    w = np.asarray(L0_attn_Wqkv)
    cols = np.arange(D).reshape(H, PAIRS, 2).transpose(2, 1, 0).reshape(-1)
    order = np.concatenate([cols, D + cols, np.arange(2 * D, 3 * D)])
    arrays = {
        "x": np.ascontiguousarray(L0_attn_x),
        "wqkv": np.ascontiguousarray(w[:, order]),
        "wo": np.ascontiguousarray(L0_attn_Wo),
        "wsg": np.ascontiguousarray(np.concatenate([np.asarray(L0_ffn_Ws1).T, np.asarray(L0_ffn_Wg).T,
                                                    np.asarray(L0_ffn_Ws3).T], axis=1)),
        "ws2": np.ascontiguousarray(np.asarray(L0_ffn_Ws2).T),
        "w13": np.ascontiguousarray(np.concatenate([np.asarray(L0_ffn_W1).transpose(0, 2, 1),
                                                    np.asarray(L0_ffn_W3).transpose(0, 2, 1)], axis=2)),
        "w2": np.ascontiguousarray(np.asarray(L0_ffn_W2).transpose(0, 2, 1)),
        "rope_cos": np.cos(angle).astype(np.float32),
        "rope_sin": np.sin(angle).astype(np.float32),
    }
    nc = bacc.Bacc("TRN2", target_bir_lowering=False, num_devices=1)
    aps = {n: nc.dram_tensor(f"in_{n}", v.shape, mybir.dt.from_np(v.dtype), kind="ExternalInput").ap()
           for n, v in arrays.items()}
    out = nc.dram_tensor("out_0", (B, S, D), F32, kind="ExternalOutput").ap()
    layer_kernel(nc, aps, out)
    r = run_bass_kernel_spmd(nc, [{f"in_{n}": v for n, v in arrays.items()}], core_ids=[0])
    return r.results[0]["out_0"]
```

```python
from contextlib import ExitStack

import concourse.bass as bass
from concourse import mybir

F32 = mybir.dt.float32
F32R = mybir.dt.float32r
BF16 = mybir.dt.bfloat16
I32 = mybir.dt.int32
U32 = mybir.dt.uint32
ALU = mybir.AluOpType
ACT = mybir.ActivationFunctionType
AX = mybir.AxisListType

P = 128
B, S, D = 16, 256, 256
H, HD = 16, 16
PAIRS = HD // 2
TPB = S // P
KT = D // P
T = B * S
NT = T // P
E, TOPK = 16, 4
G, TOPG = 4, 2
I = 176
IC = 88
NC_E = I // IC
SI = 352
NC_S = SI // IC
EPS = 1e-5
VW = 32
SLOT = HD
KB = 3 * SLOT
KA = KB + 2
TOKEN = D + E
ROW = D + E + 4
NACC = 2
WE = KT * SI + NC_E * D
NEG = -1e30
CAP = T + P
NBLK = T * TOPK // P + E - 1


class Queue:

    def __init__(self, sem):
        self.sem, self.count, self.items = sem, 0, []

    def add(self, build, waits=(), signal=True):
        self.items.append((list(waits), build, self.sem if signal else None, 1))
        if signal:
            self.count += 1
        return (self.sem, self.count)

    def dma(self, build, done, waits=()):
        self.items.append((list(waits), build, done.sem, 16))
        done.count += 16
        return (done.sem, done.count)

    def emit(self, eng):
        reached = {}
        for waits, build, sem, n in self.items:
            for w in waits:
                if w is not None and reached.get(id(w[0]), 0) < w[1]:
                    eng.wait_ge(w[0], w[1])
                    reached[id(w[0])] = w[1]
            ins = build(eng)
            if ins is not None and sem is not None:
                ins.then_inc(sem, n)


class Done:

    def __init__(self, sem):
        self.sem, self.count = sem, 0


def merge(stages):
    live = [[0, n, g] for n, g in stages]
    while live:
        s = min(live, key=lambda v: v[0] / v[1])
        try:
            next(s[2])
            s[0] += 1
        except StopIteration:
            live.remove(s)


def layer_kernel(nc, a, out):
    ctx = ExitStack()
    with ctx:
        part1 = ExitStack()

        def sb(name, shape, dt, scope=None):
            return (scope or ctx).enter_context(nc.sbuf_tensor(name, shape, dt))

        def sb1(name, shape, dt):
            return sb(name, shape, dt, part1)

        def sem(name):
            return ctx.enter_context(nc.semaphore(name))

        def done(name):
            return Done(sem(name))

        pe, act, dve, pool, sp = (Queue(sem(f"s_{n}")) for n in ("pe", "act", "dve", "pool", "sp"))

        qk_scr = nc.dram_tensor("qk_scr", (B, 2, 2, 2, P, S), F32).ap()
        rows_scr = nc.dram_tensor("rows_scr", (E * CAP, ROW), F32).ap()
        acc_scr = [nc.dram_tensor(f"acc_scr{i}", (T + P, D), F32).ap() for i in range(NACC)]

        bank = [ctx.enter_context(nc.psum_tensor(f"bank{i}", [P, 512], F32)) for i in range(8)]
        free = [[] for _ in range(8)]
        SHARED, SCORES, OUT = [0, 1, 2, 3, 4], [5, 6], [7]

        def take(idle):
            while not idle:
                yield
            return idle.pop(0)

        def give(idle, n, *readers):
            free[n] = list(readers)
            idle.append(n)

        ident = sb("ident", [P, P], F32)
        chosen = sb("chosen", [P, E], BF16)
        ones_b = sb("ones_b", [P, P], BF16)
        iota_e = sb("iota_e", [P, E], F32)
        region = sb("region", [P, E], F32)
        zero = sb("zero", [P, ROW], F32)
        ident_b = sb1("ident_b", [P, P], BF16)
        mask_b = sb1("mask_b", [P, 2, P], BF16)
        before_b = sb1("before_b", [P, P], BF16)
        half_pow = sb1("half_pow", [P, TPB], F32)
        cos_t, sin_t = sb1("cos_t", [P, S], F32), sb1("sin_t", [P, S], F32)

        def pair(name, shape, scope=part1):
            return [sb(f"{name}_{p}", shape, F32R, scope) for p in ("hi", "lo")]

        wqkv = pair("wqkv", [P, KT, 3 * D])
        wo = pair("wo", [P, KT, D])
        wsg = pair("wsg", [P, KT, 2 * SI + E])
        ws2 = pair("ws2", [IC, NC_S, D])
        wstage = sb1("wstage", [P, 2 * 3 * D], F32)

        NX, NV, NPT, NXN = 5, 3, 2, 4
        x_in = [sb1(f"x_in{i}", [P, TPB, D], F32) for i in range(NX)]
        stats = [sb1(f"stats{i}", [P, TPB, 6], F32) for i in range(2)]
        mv = [sb1(f"mv{i}", [P, TPB, 2], F32) for i in range(2)]
        veps = [sb1(f"veps{i}", [P, TPB], F32) for i in range(2)]
        rstd = [sb1(f"rstd{i}", [P, TPB], F32) for i in range(2)]
        xn = sb1("xn", [P, TPB, D], F32)
        xT = pair("xT", [P, KT, S])
        rope_a, rope_b, rope_c, rope_d = (sb1(f"rope_{x}", [P, S], F32) for x in "abcd")
        roped = sb1("roped", [P, 2, 2, S], F32)
        ropeds = pair("ropeds", [P, 2, 2, S])
        qst, kst = sb1("qst", [P, H, S], F32R), sb1("kst", [P, H, S], F32R)
        vhat = [sb1(f"vhat{i}", [P, TPB, H, VW], F32) for i in range(NV)]
        row_max = sb1("row_max", [P, TPB, H], F32)
        nmax = sb1("nmax", [H, 2, S], F32R)
        probs = [sb1(f"probs{i}", [P, 3, 4, P], F32) for i in range(NPT)]
        oT = [sb1(f"oT{i}", [P, 4, S], F32) for i in range(2)]
        rsum = sb1("rsum", [P, TPB, H], F32)
        o_sb = sb1("o_sb", [P, TPB, D], F32)
        oTn = pair("oTn", [P, KT, S])
        x1 = [sb1(f"x1_{i}", [P, TPB, D], F32) for i in range(2)]
        xn2 = [sb1(f"xn2_{i}", [P, TPB, ROW], F32) for i in range(NXN)]
        x2T = [pair(f"x2T{i}", [P, KT, S]) for i in range(2)]
        gate_t, gate_u, hid = ([sb1(f"{x}{f}", [P, I], F32) for f in range(2)] for x in ("gate_t", "gate_u", "hid"))
        hidT = [pair(f"hidT{i}", [IC, NC_S, P]) for i in range(TPB)]
        base = [sb1(f"base{i}", [P, TPB, D], F32) for i in range(2)]
        lg = [sb1(f"lg{i}", [P, TPB, E], F32) for i in range(2)]
        rows_of = [sb1(f"rows_of{i}", [P, TPB, TOPK], I32) for i in range(2)]
        lmax = sb1("lmax", [P, TPB], F32)
        lsum = sb1("lsum", [P, TPB], F32)
        score = sb1("score", [P, TPB, E], F32)
        g8 = sb1("g8", [P, TPB, 8], F32)
        gtop = sb1("gtop", [P, TPB, 8], F32)
        gidx = sb1("gidx", [P, TPB, 8], U32)
        gidf = sb1("gidf", [P, TPB, TOPG], F32)
        geq = sb1("geq", [P, TPB, TOPG, G], F32)
        gsel = sb1("gsel", [P, TPB, G], F32)
        masked = sb1("masked", [P, TPB, E], F32)
        etop = sb1("etop", [P, TPB, 8], F32)
        eidx = sb1("eidx", [P, TPB, 8], U32)
        eidf = sb1("eidf", [P, TPB, TOPK], F32)
        onehot = sb1("onehot", [P, TPB, TOPK, E], F32)
        picks = sb1("picks", [P, TPB, E], BF16)
        place = sb1("place", [P, TPB, E], F32)
        placed = sb1("placed", [P, TPB, TOPK, E], F32)

        d_const = done("d_const")
        d_zero = done("d_zero")
        d_stage = done("d_stage")
        d_x = [done(f"d_x{i}") for i in range(NX)]
        d_scr = done("d_scr")
        d_stack = [done(f"d_stack{i}") for i in range(2)]
        d_nmax = [done(f"d_nmax{i}") for i in range(2)]
        d_base = [done(f"d_base{i}") for i in range(2)]
        d_rows = [done(f"d_rows{i}") for i in range(NXN)]

        sp.dma(lambda e: e.dma_start(cos_t[:], a["rope_cos"]), d_const)
        c_rope = sp.dma(lambda e: e.dma_start(sin_t[:], a["rope_sin"]), d_const)

        def load_x(b):
            return sp.dma(lambda e: e.dma_start(x_in[b % NX][:], a["x"][b].rearrange("(i p) d -> p i d", p=P)),
                          d_x[b % NX], [x_read.get(b - NX)])

        def zero_sums():
            for i in range(NACC):
                first = T if i == 0 else 0
                rows = acc_scr[i][first:T + P].rearrange("(n p) d -> p n d", p=P)
                n = (T + P - first) // P
                sp.dma(lambda e, rows=rows, n=n: e.dma_start(
                    rows, zero[:, 0:D].rearrange("p (o d) -> p o d", o=1).to_broadcast([P, n, D])), d_zero, [z_zero])

        x_read, x_ready = {}, {}
        x_ready[0] = load_x(0)

        z_zero = pool.add(lambda e: e.memset(zero[:], 0.0))
        pool.add(lambda e: e.memset(ident[:], 0.0))
        z = pool.add(lambda e: e.memset(half_pow[:], -0.5))
        c_ident = pool.add(lambda e: e.affine_select(out=ident[:], in_=ident[:], compare_op=ALU.not_equal, fill=1.0,
                                                     base=0, pattern=[[-1, P]], channel_multiplier=1), [z])
        c_identb = dve.add(lambda e: e.tensor_copy(ident_b[:], ident[:]), [c_ident])
        pool.add(lambda e: e.memset(mask_b[:], 0.0))
        pool.add(lambda e: e.memset(ones_b[:], 1.0))
        pool.add(lambda e: e.memset(chosen[:], 0.0))
        z = pool.add(lambda e: e.memset(before_b[:], 1.0))
        pool.add(lambda e: e.affine_select(out=mask_b[:], in_=mask_b[:], compare_op=ALU.is_ge, fill=NEG,
                                           base=0, pattern=[[0, 2], [-1, P]], channel_multiplier=1), [z])
        c_masks = pool.add(lambda e: e.affine_select(out=before_b[:], in_=before_b[:], compare_op=ALU.is_gt, fill=0.0,
                                                     base=0, pattern=[[1, P]], channel_multiplier=-1), [z])
        pool.add(lambda e: e.iota(iota_e[:], pattern=[[1, E]], base=0, channel_multiplier=0,
                                  allow_small_or_imprecise_dtypes=True))
        c_iota = pool.add(lambda e: e.iota(region[:], pattern=[[CAP, E]], base=0, channel_multiplier=0,
                                           allow_small_or_imprecise_dtypes=True))
        pool.add(lambda e: e.memset(g8[:], -1.0))
        for v in xn2:
            z = pool.add(lambda e, v=v: e.memset(v[:, :, TOKEN:ROW], 0.0))
        for v in vhat:
            z = pool.add(lambda e, v=v: e.memset(v[:], 0.0))
        for v in vhat:
            c_vhat = pool.add(lambda e, v=v: e.memset(v[:, :, :, HD:HD + 1], 1.0), [z])
        c_kst = dve.add(lambda e: e.memset(kst[:].bitcast(F32), 1.0))

        def split_hi(hi, src, waits):
            return act.add(lambda e: e.activation(hi, src, ACT.Copy), waits)

        def split_lo(lo, hi, src, waits):
            return dve.add(lambda e: e.tensor_tensor(lo, src, hi.bitcast(F32), ALU.subtract), waits)

        def split(dst, src, waits_hi, waits_lo=()):
            hi, lo = dst
            t_hi = split_hi(hi, src, waits_hi)
            return t_hi, split_lo(lo, hi, src, [t_hi, *waits_lo])

        stage_free = None
        ready = {}
        for name, dst, src, rows in (("wqkv", wqkv, a["wqkv"], P), ("wo", wo, a["wo"], P), ("wsg", wsg, a["wsg"], P),
                                     ("ws2", ws2, a["ws2"], IC)):
            k, n = dst[0].shape[1], dst[0].shape[2]
            view = wstage[0:rows, 0:k * n].rearrange("p (k n) -> p k n", k=k)
            t = sp.dma(lambda e, view=view, src=src, rows=rows: e.dma_start(view, src.rearrange("(k p) n -> p k n", p=rows)),
                       d_stage, [stage_free])
            ready[name] = stage_free = split((dst[0][:], dst[1][:]), view, [t])[1]
            if name == "wqkv":
                x_ready[1] = load_x(1)
        passes = ((0, 0), (0, 1), (1, 0))

        def product(region, stationary, moving, contraction, waits, first_starts=True):
            n = 3 * contraction
            for j in range(n):
                k, (s, m) = j // 3, passes[j % 3]
                t = pe.add(lambda e, k=k, s=s, m=m, j=j: e.matmul(
                    region, stationary(s, k), moving(m, k), start=(j == 0 and first_starts), stop=(j == n - 1),
                    skip_group_check=True), waits if j == 0 else (), signal=(j == n - 1))
            return t

        def norm(x_tile, x_tok, dst, dst_free, which):
            st, m, v, r = stats[which], mv[which], veps[which], rstd[which]
            for i in range(TPB):
                t = dve.add(lambda e, i=i: e.bn_stats(st[:, i, :], x_tile[:, i, :]), [x_tok])
            yield
            for i in range(TPB):
                t2 = dve.add(lambda e, i=i: e.bn_aggr(m[:, i, :], st[:, i, :]), [t])
            yield
            t = dve.add(lambda e: e.tensor_scalar(v[:], m[:, :, 1], EPS, None, ALU.add), [t2])
            yield
            t = pool.add(lambda e: e.tensor_tensor(r[:], v[:], half_pow[:], ALU.pow), [t])
            yield
            yield
            for i in range(TPB):
                t2 = dve.add(lambda e, i=i: e.tensor_scalar(dst[:, i, 0:D], x_tile[:, i, :], m[:, i, 0:1],
                                                            r[:, i:i + 1], ALU.subtract, ALU.mult), [t, *dst_free])
            yield
            return t2

        def turned(src, src_tok, dst, dst_free):
            n = yield from take(SHARED)
            for k in range(KT):
                for i in range(TPB):
                    t = pe.add(lambda e, k=k, i=i: e.transpose(
                        bank[n][:, k * S + i * P:k * S + (i + 1) * P], src[:, i, k * P:(k + 1) * P], ident[:]),
                        [src_tok, c_ident, *free[n]], signal=(k == KT - 1 and i == TPB - 1))
            yield
            view = bank[n][:, 0:KT * S].rearrange("p (k s) -> p k s", k=KT)
            hi = split_hi(dst[0][:], view, [t, *dst_free])
            yield
            lo = split_lo(dst[1][:], dst[0][:], view, [hi])
            give(SHARED, n, lo)
            yield
            return t, lo

        def exact_sum(e, dst, src):
            with nc.allow_low_precision(reason="sums of whole numbers that the type holds exactly"):
                return e.tensor_reduce(dst, src, AX.X, ALU.add)

        q = {}

        def project(b):
            tok = yield from norm(x_in[b % NX], x_ready[b], xn, [q.get(("xn_read", b - 1))], 0)
            q["xn_read", b], xT_ready = yield from turned(xn, tok, xT, [q.get(("xT_read", b - 1))])
            for qk in range(2):
                n = yield from take(SHARED)
                for two in range(2):
                    col = (2 * qk + two) * P
                    t = product(bank[n][:, two * S:(two + 1) * S],
                                lambda s, k, col=col: wqkv[s][:, k, col:col + P],
                                lambda m, k: xT[m][:, k, :], KT, [xT_ready, ready["wqkv"], *free[n]])
                yield
                ev, od = bank[n][:, 0:S], bank[n][:, S:2 * S]
                w = [q.get(("roped_read", b - 1))]
                t1 = dve.add(lambda e, ev=ev: e.tensor_tensor(rope_a[:], ev, cos_t[:], ALU.mult),
                             [t, c_rope, q.get("rope_sub")])
                t2 = dve.add(lambda e, od=od: e.tensor_tensor(rope_b[:], od, sin_t[:], ALU.mult))
                yield
                t3 = pool.add(lambda e, qk=qk: e.tensor_tensor(roped[:, 0, qk, :], rope_a[:], rope_b[:], ALU.subtract),
                              [t2, *w])
                q["rope_sub"] = t3
                t4 = dve.add(lambda e, ev=ev: e.tensor_tensor(rope_c[:], ev, sin_t[:], ALU.mult), [q.get("rope_add")])
                t5 = dve.add(lambda e, od=od: e.tensor_tensor(rope_d[:], od, cos_t[:], ALU.mult))
                give(SHARED, n, t5)
                yield
                t6 = dve.add(lambda e, qk=qk: e.tensor_tensor(roped[:, 1, qk, :], rope_c[:], rope_d[:], ALU.add),
                             [t5, *w])
                q["rope_add"] = t6
            n = yield from take(SHARED)
            for i in range(TPB):
                t = product(bank[n][:, i * D:(i + 1) * D],
                            lambda s, k, i=i: xT[s][:, k, i * P:(i + 1) * P],
                            lambda m, k: wqkv[m][:, k, 2 * D:3 * D], KT, free[n])
            q["xT_read", b] = t
            yield
            vt = act.add(lambda e: e.activation(vhat[b % NV][:, :, :, 0:HD],
                                                bank[n][:, 0:TPB * D].rearrange("p (i h d) -> p i h d", i=TPB, h=H),
                                                ACT.Copy), [t, c_vhat, q.get(("pv", b - NV))])
            q["v", b] = vt
            give(SHARED, n, vt)
            hi = split_hi(ropeds[0][:], roped[:], [t3, t6, q.get(("scr_done", b - 1))])
            yield
            yield
            lo = split_lo(ropeds[1][:], ropeds[0][:], roped[:], [hi, q.get(("scr_done", b - 1))])
            q["roped_read", b] = lo
            for s, t in ((0, hi), (1, lo)):
                for r in range(2):
                    w = sp.dma(lambda e, s=s, r=r: e.dma_start(qk_scr[b, :, s, r].rearrange("q w t -> w q t"),
                                                              ropeds[s][:, r, :, :].bitcast(F32)), d_scr, [t])
            q["scr_done", b] = w
            o = 64 * (b % 2)
            back = [qk_scr[b, j].rearrange("s r (p h) t -> (s r p) h t", h=H) for j in range(2)]
            ws = [w, q.get(("attended", b - 2)), c_kst]
            sp.dma(lambda e: e.dma_start(qst[o:o + SLOT, :, :].bitcast(F32), back[0][0:SLOT]), d_stack[b % 2], ws)
            sp.dma(lambda e: e.dma_start(qst[o + SLOT:o + KB, :, :].bitcast(F32), back[0]), d_stack[b % 2])
            sp.dma(lambda e: e.dma_start(kst[o:o + 2 * SLOT, :, :].bitcast(F32), back[1]), d_stack[b % 2])
            q["stack", b] = sp.dma(lambda e: e.dma_start(kst[o + 2 * SLOT:o + KB, :, :].bitcast(F32), back[1][0:SLOT]),
                                   d_stack[b % 2])

        def row_maxima(b):
            o = 64 * (b % 2)
            for i in range(TPB):
                for h in range(0, H, 2):
                    n = yield from take(SHARED)
                    view = bank[n][:].rearrange("p (h k) -> p h k", h=2)
                    for j in range(2):
                        pe.add(lambda e, j=j, h=h, i=i, n=n: e.matmul(
                            bank[n][:, j * S:(j + 1) * S], qst[o:o + KB, h + j, i * P:(i + 1) * P],
                            kst[o:o + KB, h + j, :], start=(j == 0), stop=False, skip_group_check=True),
                            [q["stack", b], c_kst, *free[n]] if j == 0 else (), signal=False)
                    t = pe.add(lambda e, i=i, view=view: e.matmul(
                        view[:, :, i * P:(i + 1) * P], ident_b[:], mask_b[:], start=False, stop=True,
                        skip_group_check=True), [c_identb, c_masks])
                    yield
                    tm = dve.add(lambda e, i=i, h=h, view=view: e.tensor_reduce(
                        row_max[:, i, h:h + 2], view[:, :, 0:(i + 1) * P], AX.X, ALU.max),
                        [t, q.get(("max_turned", b - 1))])
                    give(SHARED, n, tm)
            yield
            n = yield from take(SHARED)
            for i in range(TPB):
                t = pe.add(lambda e, i=i: e.transpose(bank[n][0:H, i * P:(i + 1) * P], row_max[:, i, :], ident[:]),
                           [tm, *free[n]], signal=(i == TPB - 1))
            q["max_turned", b] = t
            yield
            hi = act.add(lambda e: e.activation(nmax[:, 0, :], bank[n][0:H, 0:S], ACT.Copy, scale=-1.0),
                         [t, q.get(("nmax_done", b - 1))])
            yield
            lo = dve.add(lambda e: e.scalar_tensor_tensor(out=nmax[:, 1, :], in0=bank[n][0:H, 0:S], scalar=-1.0,
                                                          in1=nmax[:, 0, :].bitcast(F32), op0=ALU.mult,
                                                          op1=ALU.subtract), [hi])
            give(SHARED, n, lo)
            for j in range(2):
                t = sp.dma(lambda e, j=j: e.dma_start(qst[o + KB + j:o + KB + j + 1, :, :].bitcast(F32),
                                                      nmax[:, j, :].bitcast(F32)), d_nmax[b % 2], [lo])
            q["nmax_done", b] = t

        def attend(b):
            o = 64 * (b % 2)
            pending, copy_out = None, None
            for g in range(H // 4):
                pt = probs[(4 * b + g) % NPT]
                for u in range(2):
                    exps = []
                    for kt in range(2):
                        n = yield from take(SCORES)
                        view = bank[n][:].rearrange("p (h q) -> p h q", h=2)
                        for j in range(2):
                            h = 4 * g + 2 * u + j
                            t = pe.add(lambda e, j=j, h=h, kt=kt, n=n: e.matmul(
                                bank[n][:, j * S:(j + 1) * S], kst[o:o + KA, h, kt * P:(kt + 1) * P],
                                qst[o:o + KA, h, :], start=(j == 0), stop=(j == 1), skip_group_check=True),
                                [q["nmax_done", b], q["stack", b], *free[n]], signal=(j == 1))
                        dst = (pt[:, 0:3:2, 2 * u:2 * u + 2, :].rearrange("p c h q -> p h c q") if kt == 0
                               else pt[:, 1, 2 * u:2 * u + 2, :])
                        src = (view.rearrange("p h (c q) -> p h c q", c=2) if kt == 0 else view[:, :, P:])
                        exps.append((n, dst, src, t))
                    yield
                    for n, dst, src, t in exps:
                        te = act.add(lambda e, dst=dst, src=src: e.activation(dst, src, ACT.Exp, scale=0.25),
                                     [t, q.get(("pv_read", 4 * b + g - NPT))])
                        give(SCORES, n, te)
                    if u == 0 and pending:
                        pending()
                    if u == 1 and copy_out:
                        copy_out()
                    yield
                diag = pt[:, 0:2, :, :].rearrange("p c h q -> p (c h q)")
                ts = pool.add(lambda e, diag=diag: e.affine_select(
                    out=diag, in_=diag, compare_op=ALU.is_ge, fill=0.0, base=0,
                    pattern=[[0, 8], [1, P]], channel_multiplier=-1), [te])

                def pending(g=g, pt=pt, ts=ts):
                    n, = OUT
                    for kt in range(2):
                        for j in range(4):
                            mov = pt[:, 0:3:2, j, :] if kt == 0 else pt[:, 1, j, :]
                            t = pe.add(lambda e, j=j, kt=kt, mov=mov: e.matmul(
                                bank[n][32 * j:32 * j + VW, kt * P:S], vhat[b % NV][:, kt, 4 * g + j, :], mov,
                                start=(kt == 0), stop=(kt == 1), skip_group_check=True),
                                [ts, q["v", b], *free[n]], signal=(kt == 1 and j == 3))
                    q["pv_read", 4 * b + g] = q["pv", b] = t

                def copy_out(g=g):
                    n, = OUT
                    tc = act.add(lambda e: e.activation(oT[b % 2][:, g, :], bank[n][:, 0:S], ACT.Copy),
                                 [q["pv_read", 4 * b + g], q.get(("oT_read", b - 2))])
                    free[n] = [tc]
                    q["oT", b] = tc
            q["attended", b] = t
            yield
            pending()
            yield
            copy_out()

        def mix(b):
            x2 = xn2[b % NXN]
            for i in range(TPB):
                n = yield from take(SHARED)
                for g in range(4):
                    t = pe.add(lambda e, g=g, i=i, n=n: e.transpose(
                        bank[n][:, g * P:(g + 1) * P], oT[b % 2][:, g, i * P:(i + 1) * P], ident[:]),
                        [q["oT", b], *free[n]], signal=(g == 3))
                yield
                heads = bank[n][:].rearrange("p (h w) -> p h w", w=VW)
                tr = dve.add(lambda e, i=i, heads=heads: e.reciprocal(rsum[:, i, :], heads[:, :, HD]), [t])
                to = dve.add(lambda e, i=i, heads=heads: e.tensor_tensor(
                    o_sb[:, i, :].rearrange("p (h d) -> p h d", h=H), heads[:, :, 0:HD],
                    rsum[:, i, :].rearrange("p (h o) -> p h o", o=1).to_broadcast([P, H, HD]), ALU.mult),
                    [tr, q.get(("o_read", b - 1))])
                give(SHARED, n, to)
            yield
            q["oT_read", b] = t
            q["o_read", b], oTn_ready = yield from turned(o_sb, to, oTn, [q.get(("oTn_read", b - 1))])
            n = yield from take(SHARED)
            for i in range(TPB):
                t = product(bank[n][:, i * D:(i + 1) * D], lambda s, k, i=i: oTn[s][:, k, i * P:(i + 1) * P],
                            lambda m, k: wo[m][:, k, :], KT, [oTn_ready, ready["wo"], *free[n]])
            q["oTn_read", b] = t
            yield
            t1 = dve.add(lambda e, n=n: e.tensor_tensor(x1[b % 2][:].rearrange("p i d -> p (i d)"),
                                                        bank[n][:, 0:TPB * D],
                                                        x_in[b % NX][:].rearrange("p i d -> p (i d)"), ALU.add),
                         [t, q.get(("x1_read", b - 2))])
            give(SHARED, n, t1)
            x_read[b] = t1
            yield
            tn = yield from norm(x1[b % 2], t1, x2, [q.get(("rows_done", b - NXN)), q.get(("x2_turned", b - NXN))], 1)
            q["x2_turned", b], q["x2T", b] = yield from turned(x2, tn, x2T[b % 2], [q.get(("x2T_read", b - 2))])
            q["x2", b] = tn

        def shared_tile(b, i):
            for f in range(2):
                n = yield from take(SHARED)
                c0, width = ((0, 2 * I + E), (2 * I + E, 2 * I))[f]
                ta = product(bank[n][:, 0:width], lambda s, k: x2T[b % 2][s][:, k, i * P:(i + 1) * P],
                             lambda m, k, c0=c0, width=width: wsg[m][:, k, c0:c0 + width], KT,
                             [q["x2T", b], ready["wsg"], *free[n]])
                q["x2T_read", b] = ta
                yield
                tt = act.add(lambda e, n=n: e.activation(gate_t[i][:], bank[n][:, 0:I], ACT.Tanh, scale=0.5),
                             [ta, q.get(("gate_read", i))])
                if f == 0:
                    tt = act.add(lambda e, n=n: e.activation(lg[b % 2][:, i, :], bank[n][:, 2 * I:2 * I + E],
                                                             ACT.Copy), [q.get(("lg_read", b - 2))])
                    q["lg", b, i] = tt
                yield
                tu = dve.add(lambda e, n=n: e.scalar_tensor_tensor(
                    out=gate_u[i][:], in0=gate_t[i][:], scalar=1.0, in1=bank[n][:, 0:I], op0=ALU.add,
                    op1=ALU.mult), [tt])
                q["gate_read", i] = tu
                th = dve.add(lambda e, n=n: e.scalar_tensor_tensor(
                    out=hid[i][:], in0=gate_u[i][:], scalar=0.5, in1=bank[n][:, I:2 * I], op0=ALU.mult,
                    op1=ALU.mult), [tu, q.get(("hid_read", i))])
                give(SHARED, n, th)
                yield
                n = yield from take(SHARED)
                for c in range(2):
                    t = pe.add(lambda e, c=c, n=n: e.transpose(bank[n][0:IC, c * P:(c + 1) * P],
                                                               hid[i][:, c * IC:(c + 1) * IC], ident[:]),
                               [th, *free[n]], signal=(c == 1))
                q["hid_read", i] = t
                yield
                view = bank[n][0:IC, 0:2 * P].rearrange("p (c t) -> p c t", c=2)
                dst = [u[:, 2 * f:2 * f + 2, :] for u in hidT[i]]
                hi = split_hi(dst[0], view, [t, q.get(("hidT_read", i))])
                yield
                lo = split_lo(dst[1], dst[0], view, [hi])
                give(SHARED, n, lo)
            yield
            n = yield from take(SHARED)
            t = product(bank[n][:, 0:D], lambda s, k: hidT[i][s][:, k, :], lambda m, k: ws2[m][:, k, :], NC_S,
                        [lo, ready["ws2"], *free[n]])
            q["hidT_read", i] = t
            yield
            tbase = dve.add(lambda e, n=n: e.tensor_tensor(base[b % 2][:, i, :], bank[n][:, 0:D], x1[b % 2][:, i, :],
                                                           ALU.add), [t, q.get(("base_done", b - 2))])
            give(SHARED, n, tbase)
            q["x1_read", b] = tbase

        def shared(b):
            first, second = shared_tile(b, 0), shared_tile(b, 1)
            for _ in range(3):
                next(first)
                yield
            live = [second, first]
            while live:
                for g in list(live):
                    try:
                        next(g)
                    except StopIteration:
                        live.remove(g)
                yield
            q["base_done", b] = sp.dma(lambda e: e.dma_start(
                acc_scr[0][b * S:(b + 1) * S].rearrange("(i p) d -> p i d", p=P), base[b % 2][:]), d_base[b % 2],
                [q["x1_read", b]])

        def route(b):
            x2, logits = xn2[b % NXN], lg[b % 2]

            def v(build, *waits):
                return dve.add(build, waits)

            def bc(ap, shape):
                return ap.to_broadcast(shape)
            t = v(lambda e: e.tensor_reduce(lmax[:], logits[:], AX.X, ALU.max), q["lg", b, 0], q["lg", b, 1])
            yield
            t = v(lambda e: e.tensor_tensor(logits[:], logits[:],
                                            bc(lmax[:].rearrange("p (i o) -> p i o", o=1), [P, TPB, E]),
                                            ALU.subtract), t)
            yield
            t = act.add(lambda e: e.activation(logits[:], logits[:], ACT.Exp), [t])
            tt = pool.add(lambda e: e.iota(x2[:, :, TOKEN:TOKEN + 1].bitcast(I32), pattern=[[P, TPB], [1, 1]],
                                           base=b * S, channel_multiplier=1), [q["x2", b]])
            yield
            t = v(lambda e: e.tensor_reduce(lsum[:], logits[:], AX.X, ALU.add), t)
            yield
            t = v(lambda e: e.reciprocal(lsum[:], lsum[:]), t)
            yield
            t = v(lambda e: e.tensor_tensor(score[:], logits[:], bc(lsum[:].rearrange("p (i o) -> p i o", o=1),
                                                                   [P, TPB, E]), ALU.mult), t)
            q["lg_read", b] = t
            yield
            by_group = score[:].rearrange("p i (g m) -> p i g m", g=G)
            t = v(lambda e: e.tensor_reduce(g8[:, :, 0:G], by_group, AX.X, ALU.max), t, c_iota)
            yield
            for i in range(TPB):
                t = v(lambda e, i=i: e.max(gtop[:, i, :], g8[:, i, :]), t)
            yield
            for i in range(TPB):
                t = v(lambda e, i=i: e.max_index(gidx[:, i, :], gtop[:, i, :], g8[:, i, :]), t)
            yield
            t = v(lambda e: e.tensor_copy(gidf[:], gidx[:, :, 0:TOPG]), t)
            yield
            full = [P, TPB, TOPG, G]
            t = v(lambda e: e.tensor_tensor(
                geq[:], bc(iota_e[:, 0:G].rearrange("p (i k g) -> p i k g", i=1, k=1), full),
                bc(gidf[:].rearrange("p i (k o) -> p i k o", o=1), full), ALU.is_equal), t)
            yield
            t = v(lambda e: e.tensor_tensor(gsel[:], geq[:, :, 0, :], geq[:, :, 1, :], ALU.add), t)
            yield
            selb = bc(gsel[:].rearrange("p i (g o) -> p i g o", o=1), [P, TPB, G, E // G])
            mview = masked[:].rearrange("p i (g m) -> p i g m", g=G)
            t = v(lambda e: e.tensor_tensor(mview, by_group, selb, ALU.mult), t)
            yield
            t = v(lambda e: e.scalar_tensor_tensor(out=mview, in0=selb, scalar=-1.0, in1=mview, op0=ALU.add,
                                                   op1=ALU.add), t)
            yield
            for i in range(TPB):
                t = v(lambda e, i=i: e.max(etop[:, i, :], masked[:, i, :]), t)
            yield
            for i in range(TPB):
                t = v(lambda e, i=i: e.max_index(eidx[:, i, :], etop[:, i, :], masked[:, i, :]), t)
            yield
            t = v(lambda e: e.tensor_copy(eidf[:], eidx[:, :, 0:TOPK]), t)
            yield
            full2 = [P, TPB, TOPK, E]
            t = v(lambda e: e.tensor_tensor(
                onehot[:], bc(iota_e[:].rearrange("p (i k e) -> p i k e", i=1, k=1), full2),
                bc(eidf[:].rearrange("p i (k o) -> p i k o", o=1), full2), ALU.is_equal), t)
            yield
            t = v(lambda e: exact_sum(e, picks[:], onehot[:].rearrange("p i k e -> p i e k")), t,
                  q.get(("ranked", b - 1)), q.get(("chosen", b - 1)))
            yield
            tw = v(lambda e: e.tensor_tensor(x2[:, :, D:D + E], score[:], picks[:], ALU.mult), t)
            n = yield from take(SHARED)
            pe.add(lambda e: e.matmul(bank[n][:, 0:E], before_b[:], picks[:, 0, :], start=True, stop=False,
                                      skip_group_check=True), [t, q.get(("chosen", b - 1)), c_masks, *free[n]],
                   signal=False)
            pe.add(lambda e: e.matmul(bank[n][:, 0:E], ones_b[:], chosen[:], start=False, stop=True,
                                      skip_group_check=True), (), signal=False)
            pe.add(lambda e: e.matmul(bank[n][:, E:2 * E], before_b[:], picks[:, 1, :], start=False, stop=False,
                                      skip_group_check=True), (), signal=False)
            pe.add(lambda e: e.matmul(bank[n][:, E:2 * E], ones_b[:], picks[:, 0, :], start=False, stop=False,
                                      skip_group_check=True), (), signal=False)
            t2 = pe.add(lambda e: e.matmul(bank[n][:, E:2 * E], ones_b[:], chosen[:], start=False, stop=True,
                                           skip_group_check=True))
            q["ranked", b] = t2
            t = v(lambda e: e.tensor_tensor(place[:], bank[n][:, 0:TPB * E].rearrange("p (i e) -> p i e", i=TPB),
                                            bc(region[:].rearrange("p (i e) -> p i e", i=1), [P, TPB, E]), ALU.add), t2)
            give(SHARED, n, t)
            t3 = pool.add(lambda e: e.tensor_tensor(chosen[:], chosen[:], picks[:, 0, :], ALU.add), [t2])
            q["chosen", b] = pool.add(lambda e: e.tensor_tensor(chosen[:], chosen[:], picks[:, 1, :], ALU.add), [t3])
            yield
            t = v(lambda e: e.tensor_tensor(placed[:], onehot[:], bc(place[:].rearrange("p i (k e) -> p i k e", k=1),
                                                                     full2), ALU.mult), t)
            yield
            t = v(lambda e: exact_sum(e, rows_of[b % 2][:], placed[:]), t, q.get(("rows_done", b - 2)))
            yield
            for i in range(TPB):
                for k in range(TOPK):
                    w = pool.dma(lambda e, i=i, k=k: e.indirect_dma_start(
                        rows_scr[:, :], bass.IndirectOffsetOnAxis(ap=rows_of[b % 2][:, i, k:k + 1].bitcast(U32),
                                                                  axis=0), x2[:, i, :], None), d_rows[b % NXN],
                        [t, tt, tw])
                    if k % 2:
                        yield
            q["rows_done", b] = w

        part1.close()
        LAST = B
        for s in range(LAST + 5):
            merge([(n, stage(s - lag)) for lag, n, stage in
                   ((2, 18, attend), (1, 21, row_maxima), (0, 20, project), (3, 22, mix), (4, 20, shared),
                    (5, 28, route))
                   if 0 <= s - lag < LAST])
            if s + 2 < LAST:
                x_ready[s + 2] = load_x(s + 2)
            if s == 1:
                zero_sums()
        over = [(u.sem, u.count) for u in (pe, act, dve, pool)]
        over += [(u.sem, u.count) for u in (d_const, d_stage, d_scr, *d_x, *d_stack, *d_nmax, *d_base, *d_rows)]
        part2 = ExitStack()

        def sb2(name, shape, dt):
            return sb(name, shape, dt, part2)

        LOADS = 4
        NXB, NYB, NST, NW = 5, 3, 2, 6
        wexp = pair("wexp", [P, E * WE], part2)
        st = [sb2(f"st{i}", [P, WE], F32) for i in range(NST)]
        xb = [sb2(f"xb{i}", [P, ROW], F32) for i in range(NXB)]
        xbT = [pair(f"xbT{i}", [P, KT, P], part2) for i in range(2)]
        silu = sb2("silu", [P, I], F32)
        up = [sb2(f"up{i}", [P, I], F32) for i in range(2)]
        upT = [pair(f"upT{i}", [IC, NC_E, P], part2) for i in range(2)]
        yb = [sb2(f"yb{i}", [P, D], F32) for i in range(NYB)]
        picked = sb2("picked", [P, E], F32)
        weight = [sb2(f"weight{i}", [P, 1], F32) for i in range(NW)]
        token = [sb2(f"token{i}", [P, 1], I32) for i in range(NW)]
        cnt = sb2("cnt", [P, E], F32)
        tail = sb2("tail", [P, E], I32)
        lane = sb2("lane", [P, E], F32)
        nblk_i = sb2("nblk_i", [P, E], I32)
        nblk = sb2("nblk", [P, E], F32)
        zrow = sb2("zrow", [P, E], F32)
        ends = sb2("ends", [P, E], F32)
        wide = sb2("wide", [P, NBLK, E], F32)
        blk = sb2("blk", [P, NBLK], F32)
        real = sb2("real", [P, NBLK], F32)
        expert = sb2("expert", [P, NBLK], F32)
        row_f = sb2("row_f", [P, NBLK], F32)
        row_t = sb2("row_t", [P, NBLK], I32)
        off_t = sb2("off_t", [P, NBLK], I32)
        d_tail = done("d_tail")
        d_w = [done(f"d_w{i}") for i in range(NST)]
        d_xb = [done(f"d_xb{i}") for i in range(NXB)]
        d_add = [done(f"d_add{i}") for i in range(NACC)]

        n = 0
        tc = pe.add(lambda e: e.matmul(bank[n][:, 0:E], ones_b[:], chosen[:], start=True, stop=True),
                    [q["chosen", LAST - 1], *free[n]])
        tz = pool.add(lambda e: e.iota(zero[:, TOKEN:TOKEN + 1].bitcast(I32), pattern=[[1, 1]], base=T,
                                       channel_multiplier=1), [(d_zero.sem, d_zero.count), *over])
        pool.add(lambda e: e.memset(zrow[:], 0.0))
        pool.add(lambda e: e.iota(blk[:], pattern=[[1, NBLK]], base=0, channel_multiplier=0,
                                  allow_small_or_imprecise_dtypes=True))
        tl = pool.add(lambda e: e.iota(lane[:], pattern=[[CAP, E]], base=0, channel_multiplier=1,
                                       allow_small_or_imprecise_dtypes=True))

        def v(build, *waits):
            return dve.add(build, waits)

        t = v(lambda e: e.tensor_copy(cnt[:], bank[n][:, 0:E]), tc, *over)
        free[n] = [t]
        t2 = v(lambda e: e.tensor_tensor(tail[:], cnt[:], lane[:], ALU.add), t, tl)
        for x in range(E):
            w_tail = pool.dma(lambda e, x=x: e.indirect_dma_start(
                rows_scr[:, :], bass.IndirectOffsetOnAxis(ap=tail[:, x:x + 1].bitcast(U32), axis=0), zero[:], None),
                d_tail, [t2, tz])
        t = v(lambda e: e.tensor_scalar(nblk_i[:], cnt[:], P / 2 - 0.5, 1.0 / P, ALU.add, ALU.mult), t2)
        t = v(lambda e: e.tensor_copy(nblk[:], nblk_i[:]), t)
        t = v(lambda e: e.tensor_tensor_scan(ends[:], nblk[:], zrow[:], 0.0, ALU.add, ALU.add), t)
        total = ends[:, E - 1:E]
        t1 = v(lambda e: e.tensor_scalar(row_f[:], blk[:], total, total, ALU.is_ge, ALU.mult), t)
        t = v(lambda e: e.tensor_scalar(real[:], blk[:], total, None, ALU.is_lt), t1)
        t = v(lambda e: e.tensor_tensor(blk[:], blk[:], row_f[:], ALU.subtract), t)

        def per_block(ap):
            return ap.rearrange("p (b o) -> p b o", o=1).to_broadcast([P, NBLK, E])

        def per_e(ap):
            return ap.rearrange("p (o e) -> p o e", o=1).to_broadcast([P, NBLK, E])
        t = v(lambda e: e.tensor_tensor(wide[:], per_block(blk[:]), per_e(ends[:]), ALU.is_ge), t)
        t = v(lambda e: e.tensor_reduce(expert[:], wide[:], AX.X, ALU.add), t)
        t_off = v(lambda e: e.tensor_scalar(off_t[:], expert[:], float(WE), None, ALU.mult), t)
        t = v(lambda e: e.tensor_tensor(wide[:], wide[:], per_e(nblk[:]), ALU.mult), t_off)
        t = v(lambda e: e.tensor_reduce(row_f[:], wide[:], AX.X, ALU.add), t)
        t = v(lambda e: e.tensor_tensor(row_f[:], blk[:], row_f[:], ALU.subtract), t)
        t = v(lambda e: e.tensor_scalar(row_f[:], row_f[:], float(P), None, ALU.mult), t)
        t_row = v(lambda e: e.scalar_tensor_tensor(out=row_t[:], in0=expert[:], scalar=float(CAP), in1=row_f[:],
                                                   op0=ALU.mult, op1=ALU.add), t)
        t = v(lambda e: e.tensor_tensor(wide[:], per_block(expert[:]), per_e(iota_e[:]), ALU.is_equal), t_row)
        t_wide = v(lambda e: e.tensor_tensor(wide[:], wide[:], per_block(real[:]), ALU.mult), t)

        st_free = [None] * NST
        for x in range(E):
            i = x % NST
            t = sp.dma(lambda e, x=x, i=i: e.dma_start(st[i][:], a["wexp"][x]), d_w[i], [st_free[i], *over])
            st_free[i] = split([w[:, x * WE:(x + 1) * WE] for w in wexp], st[i][:], [t])[1]
        weights_ready = st_free[(E - 1) % NST]

        r = {}
        regs = {}

        def fetch(queue, key, table, top, waits):
            def build(e):
                regs[key] = e.value_load(table, min_val=0, max_val=top)
            queue.add(build, waits, signal=False)

        def load_rows(j):
            fetch(sp, ("x", j), row_t[0:1, j:j + 1], E * CAP - P, [t_row])
            r["x", j] = sp.dma(lambda e: e.dma_start(xb[j % NXB][:], rows_scr[bass.ds(regs["x", j], P), :]),
                               d_xb[j % NXB], [(d_tail.sem, d_tail.count), *((d.sem, d.count) for d in d_rows),
                                               *r.get(("x_read", j - NXB), ())])

        def turn_rows(j):
            n = (0, 1)[j % 2]
            x = xb[j % NXB]
            for k in range(KT):
                t = pe.add(lambda e, k=k: e.transpose(bank[n][:, k * P:(k + 1) * P], x[:, k * P:(k + 1) * P],
                                                      ident[:]), [r["x", j], *free[n]], signal=(k == KT - 1))
            t1 = dve.add(lambda e: e.tensor_copy(token[j % NW][:], x[:, TOKEN:TOKEN + 1].bitcast(I32)),
                         [r["x", j], r.get(("add", j - NW))])
            t2 = dve.add(lambda e: e.tensor_tensor(picked[:], x[:, D:D + E], wide[:, j, :], ALU.mult),
                         [t_wide, r.get(("weight", j - 1))])
            r["x_read", j] = [t, t2]
            hi, lo = split([u[:] for u in xbT[j % 2]], bank[n][:, 0:KT * P].rearrange("p (k t) -> p k t", k=KT),
                           [t, r.get(("xT_read", j - 2))])
            r["weight", j] = dve.add(lambda e: e.tensor_reduce(weight[j % NW][:], picked[:], AX.X, ALU.add),
                                     [t2, r.get(("y", j - NW))])
            free[n] = [lo]
            r["xT", j] = lo

        def hidden(j):
            n = (2, 3)[j % 2]
            t = product(bank[n][:, 0:SI], lambda s, k: xbT[j % 2][s][:, k, :],
                        lambda m, k: wexp[m][:, bass.ds(regs["w", j] + k * SI, SI)], KT,
                        [r["xT", j], weights_ready, *free[n]])
            if j + 1 < NBLK and (j + 1) % LOADS == 0:
                fetch_weights(j + 1)
            r["xT_read", j] = t
            t = act.add(lambda e: e.activation(silu[:], bank[n][:, 0:I], ACT.Silu), [t, r.get("silu_read")])
            t = dve.add(lambda e: e.tensor_tensor(up[j % 2][:], silu[:], bank[n][:, I:SI], ALU.mult),
                        [t, r.get(("up_read", j - 2))])
            r["silu_read"] = r["up", j] = t
            free[n] = [t]

        def fetch_weights(j):
            js = range(j, min(j + LOADS, NBLK))

            def build(e):
                offsets = [e.alloc_register(f"offset{j_ % (2 * LOADS)}_{j_}") for j_ in js]
                e.load(offsets, off_t[0:1, j:j + len(js)])
                for j_, reg in zip(js, offsets):
                    regs["w", j_] = e.snap(reg, min_val=0, max_val=(E - 1) * WE)
            pe.add(build, [t_off], signal=False)

        def turn_hidden(j):
            n = (4, 5)[j % 2]
            for c in range(NC_E):
                t = pe.add(lambda e, c=c: e.transpose(bank[n][0:IC, c * P:(c + 1) * P],
                                                      up[j % 2][:, c * IC:(c + 1) * IC], ident[:]),
                           [r["up", j], *free[n]], signal=(c == NC_E - 1))
            r["up_read", j] = t
            hi, lo = split([u[:] for u in upT[j % 2]], bank[n][0:IC, 0:NC_E * P].rearrange("p (c t) -> p c t", c=NC_E),
                           [t, r.get(("upT_read", j - 2))])
            free[n] = [lo]
            r["upT", j] = lo

        def result(j):
            n = (6, 7)[j % 2]
            t = product(bank[n][:, 0:D], lambda s, k: upT[j % 2][s][:, k, :],
                        lambda m, k: wexp[m][0:IC, bass.ds(regs["w", j] + KT * SI + k * D, D)], NC_E,
                        [r["upT", j], *free[n]])
            r["upT_read", j] = t
            t = act.add(lambda e: e.activation(yb[j % NYB][:], bank[n][:, 0:D], ACT.Copy, scale=weight[j % NW][:]),
                        [t, r["weight", j], r.get(("add", j - NYB))])
            free[n] = [t]
            r["y", j] = t
            r["add", j] = pool.dma(lambda e: e.indirect_dma_start(
                acc_scr[j % NACC][:, :], bass.IndirectOffsetOnAxis(ap=token[j % NW][:].bitcast(U32), axis=0),
                yb[j % NYB][:], None, compute_op=ALU.add), d_add[j % NACC],
                [t, r.get(("add", j - NACC)), (d_zero.sem, d_zero.count), *((d.sem, d.count) for d in d_base)])

        for j in range(NXB - 1):
            load_rows(j)
        fetch_weights(0)
        for s in range(NBLK + 3):
            if s < NBLK:
                turn_rows(s)
            if s + NXB - 1 < NBLK:
                load_rows(s + NXB - 1)
            if 0 <= s - 1 < NBLK:
                hidden(s - 1)
            if 0 <= s - 2 < NBLK:
                turn_hidden(s - 2)
            if 0 <= s - 3 < NBLK:
                result(s - 3)

        part2.close()
        part3 = ExitStack()
        NF, TF = 4, 4
        acc = [[sb(f"acc{i}_{k}", [P, TF, D], F32, part3) for k in range(NACC)] for i in range(NF)]
        d_acc = [done(f"d_acc{i}") for i in range(NF)]
        d_out = [done(f"d_out{i}") for i in range(NF)]
        added = [(d.sem, d.count) for d in d_add] + [(u.sem, u.count) for u in (pe, act, dve, pool)]
        out_rows = out.rearrange("b s d -> (b s) d")
        for f in range(NT // TF):
            i = f % NF
            rows = slice(f * TF * P, (f + 1) * TF * P)
            for k in range(NACC):
                t = (sp, act)[k].dma(lambda e, i=i, k=k, rows=rows: e.dma_start(
                    acc[i][k][:], acc_scr[k][rows, :].rearrange("(p n) d -> p n d", n=TF)), d_acc[i],
                    [r.get(("out", f - NF)), *added])
            t = dve.add(lambda e, i=i: e.tensor_tensor(acc[i][0][:], acc[i][0][:], acc[i][1][:], ALU.add), [t])
            r["out", f] = sp.dma(lambda e, i=i, rows=rows: e.dma_start(
                out_rows[rows, :].rearrange("(p n) d -> p n d", n=TF), acc[i][0][:]), d_out[i], [t])
        part3.close()

        finish(nc, ctx, (sp, act, dve, pool, pe), [d_scr, d_zero, *d_base, *d_rows, d_tail, *d_add, *d_out])


def finish(nc, ctx, queues, dones):
    sp, act, dve, pool, pe = queues
    with nc.Block() as block:
        @block.sync
        def _(eng):
            sp.emit(eng)
            for d in dones:
                if d.count:
                    eng.wait_ge(d.sem, d.count)

        @block.scalar
        def _(eng):
            act.emit(eng)

        @block.vector
        def _(eng):
            dve.emit(eng)

        @block.gpsimd
        def _(eng):
            pool.emit(eng)

        @block.tensor
        def _(eng):
            pe.emit(eng)


def kernel(L0_attn_x, L0_attn_Wqkv, L0_attn_Wo, L0_ffn_Wg, L0_ffn_W1, L0_ffn_W3, L0_ffn_W2, L0_ffn_Ws1, L0_ffn_Ws3,
           L0_ffn_Ws2):
    import numpy as np
    import concourse.bacc as bacc
    from concourse.bass_utils import run_bass_kernel_spmd

    inv = (1.0 / 10000.0 ** (2.0 * np.arange(PAIRS, dtype=np.float32) / HD)).astype(np.float32)
    angle = np.repeat(np.outer(inv, np.arange(S, dtype=np.float32)).astype(np.float32), H, axis=0)
    w = np.asarray(L0_attn_Wqkv)
    cols = np.arange(D).reshape(H, PAIRS, 2).transpose(2, 1, 0).reshape(-1)
    order = np.concatenate([cols, D + cols, np.arange(2 * D, 3 * D)])
    s1, s3 = np.asarray(L0_ffn_Ws1).T, np.asarray(L0_ffn_Ws3).T
    w1, w3, w2 = (np.asarray(v).transpose(0, 2, 1) for v in (L0_ffn_W1, L0_ffn_W3, L0_ffn_W2))
    wexp = np.zeros((E, P, WE), np.float32)
    wexp[:, :, :KT * SI] = (np.concatenate([w1, w3], axis=2).reshape(E, KT, P, SI).transpose(0, 2, 1, 3)
                            .reshape(E, P, KT * SI))
    wexp[:, :IC, KT * SI:] = w2.reshape(E, NC_E, IC, D).transpose(0, 2, 1, 3).reshape(E, IC, NC_E * D)
    arrays = {
        "x": np.ascontiguousarray(L0_attn_x),
        "wqkv": np.ascontiguousarray(w[:, order]),
        "wo": np.ascontiguousarray(L0_attn_Wo),
        "wsg": np.ascontiguousarray(np.concatenate([s1[:, :I], s3[:, :I], np.asarray(L0_ffn_Wg).T, s1[:, I:], s3[:, I:]],
                                                   axis=1)),
        "ws2": np.ascontiguousarray(np.asarray(L0_ffn_Ws2).T),
        "wexp": wexp,
        "rope_cos": np.cos(angle).astype(np.float32),
        "rope_sin": np.sin(angle).astype(np.float32),
    }
    nc = bacc.Bacc("TRN2", target_bir_lowering=False, num_devices=1)
    aps = {n: nc.dram_tensor(f"in_{n}", v.shape, mybir.dt.from_np(v.dtype), kind="ExternalInput").ap()
           for n, v in arrays.items()}
    out = nc.dram_tensor("out_0", (B, S, D), F32, kind="ExternalOutput").ap()
    layer_kernel(nc, aps, out)
    r = run_bass_kernel_spmd(nc, [{f"in_{n}": v for n, v in arrays.items()}], core_ids=[0])
    return r.results[0]["out_0"]
```

```python
from contextlib import ExitStack

import concourse.bass as bass
from concourse import mybir

F32 = mybir.dt.float32
F32R = mybir.dt.float32r
BF16 = mybir.dt.bfloat16
I32 = mybir.dt.int32
U32 = mybir.dt.uint32
ALU = mybir.AluOpType
ACT = mybir.ActivationFunctionType
AX = mybir.AxisListType

P = 128
B, S, D = 16, 256, 256
H, HD = 16, 16
PAIRS = HD // 2
TPB = S // P
KT = D // P
T = B * S
NT = T // P
E, TOPK = 16, 4
G, TOPG = 4, 2
I = 176
IC = 88
NC_E = I // IC
SI = 352
NC_S = SI // IC
EPS = 1e-5
VW = 32
HALVES = (slice(0, H // 2), slice(H // 2, H))
SLOT = HD
KB = 3 * SLOT
KA = KB + 2
TOKEN = D + E
ROW = D + E + 4
NACC = 2
WE = KT * SI + NC_E * D
NEG = -1e30
CAP = T + P
NBLK = T * TOPK // P + E - 1


class Queue:

    def __init__(self, sem):
        self.sem, self.count, self.items = sem, 0, []

    def add(self, build, waits=(), signal=True):
        self.items.append((list(waits), build, self.sem if signal else None, 1))
        if signal:
            self.count += 1
        return (self.sem, self.count)

    def dma(self, build, done, waits=()):
        self.items.append((list(waits), build, done.sem, 16))
        done.count += 16
        return (done.sem, done.count)

    def emit(self, eng):
        reached = {}
        for waits, build, sem, n in self.items:
            for w in waits:
                if w is not None and reached.get(id(w[0]), 0) < w[1]:
                    eng.wait_ge(w[0], w[1])
                    reached[id(w[0])] = w[1]
            ins = build(eng)
            if ins is not None and sem is not None:
                ins.then_inc(sem, n)


class Done:

    def __init__(self, sem):
        self.sem, self.count = sem, 0


def merge(runs):
    live = [[start, order, (end - start) / steps, g] for order, (start, end, steps, g) in enumerate(runs)]
    while live:
        run = min(live, key=lambda v: v[:2])
        try:
            next(run[3])
            run[0] += run[2]
        except StopIteration:
            live.remove(run)


def layer_kernel(nc, a, out):
    ctx = ExitStack()
    with ctx:
        part1 = ExitStack()

        used = [0]

        def sb(name, shape, dt, scope=None):
            if scope is part1:
                n = 2 if dt is BF16 else 4
                for v in shape[1:]:
                    n *= v
                used[0] += n
            return (scope or ctx).enter_context(nc.sbuf_tensor(name, shape, dt))

        def sb1(name, shape, dt):
            return sb(name, shape, dt, part1)

        def sem(name):
            return ctx.enter_context(nc.semaphore(name))

        def done(name):
            return Done(sem(name))

        pe, act, dve, pool, sp = (Queue(sem(f"s_{n}")) for n in ("pe", "act", "dve", "pool", "sp"))

        qk_scr = nc.dram_tensor("qk_scr", (B, 2, 2, 2, P, S), F32).ap()
        rows_scr = nc.dram_tensor("rows_scr", (E * CAP, ROW), F32).ap()
        acc_scr = [nc.dram_tensor(f"acc_scr{i}", (T + P, D), F32).ap() for i in range(NACC)]

        bank = [ctx.enter_context(nc.psum_tensor(f"bank{i}", [P, 512], F32)) for i in range(8)]
        free = [[] for _ in range(8)]
        SHARED, SCORES, OUT = [0, 1, 2, 3, 4], [5, 6], [7]

        def take(idle):
            while not idle:
                yield
            return idle.pop(0)

        def give(idle, n, *readers):
            free[n] = list(readers)
            idle.append(n)

        ident = sb("ident", [P, P], F32)
        chosen = sb("chosen", [P, E], BF16)
        ones_b = sb("ones_b", [P, P], BF16)
        iota_e = sb("iota_e", [P, E], F32)
        region = sb("region", [P, E], F32)
        zero = sb("zero", [P, ROW], F32)
        half_pow = sb("half_pow", [P, TPB], F32)
        before_b = sb("before_b", [P, P], BF16)
        upto_b = sb("upto_b", [E, E], BF16)

        tail = sb("tail", [1, E], I32)
        nblk_i = sb("nblk_i", [E, P], I32)
        nblk = sb("nblk", [E, P], BF16)
        ends = sb("ends", [E, 1], F32)
        total = sb("total", [P, 1], F32)
        past_b = sb("past_b", [E, NBLK], BF16)
        blk = sb("blk", [P, NBLK], F32)
        wrap = sb("wrap", [P, NBLK], F32)
        beyond = sb("beyond", [P, NBLK], F32)
        expert = sb("expert", [P, NBLK], F32)
        picks_of = sb("picks_of", [P, NBLK], F32)
        row_f = sb("row_f", [P, NBLK], F32)
        row_t = sb("row_t", [P, NBLK], I32)
        off_t = sb("off_t", [P, NBLK], I32)

        def pair(name, shape, scope=part1):
            return [sb(f"{name}_{p}", shape, F32R, scope) for p in ("hi", "lo")]

        NX, NV, NPT, NXN = 5, 3, 2, 4
        wqkv = pair("wqkv", [P, KT, 3 * D])
        wstage = sb1("wstage", [P, 2 * 3 * D], F32)
        cos_t, sin_t = sb1("cos_t", [P, S], F32), sb1("sin_t", [P, S], F32)
        ident_b = sb1("ident_b", [P, P], BF16)
        mask_b = sb1("mask_b", [P, 2, P], BF16)
        xn = sb1("xn", [P, TPB, D], F32)
        xT = pair("xT", [P, KT, S])
        rope_a, rope_b, rope_c, rope_d = (sb1(f"rope_{x}", [P, S], F32) for x in "abcd")
        roped = sb1("roped", [P, 2, 2, S], F32)
        ropeds = pair("ropeds", [P, 2, 2, S])
        qst, kst = sb1("qst", [P, H, S], F32R), sb1("kst", [P, H, S], F32R)
        vhat = [sb1(f"vhat{i}", [P, TPB, H, VW], F32) for i in range(NV)]
        row_max = sb1("row_max", [P, TPB, H], F32)
        nmax = sb1("nmax", [H // 2, 2, 2, S], F32R)
        probs = [sb1(f"probs{i}", [P, 3, 4, P], F32) for i in range(NPT)]
        until_attended = used[0]
        oT = [sb1(f"oT{i}", [P, 4, S], F32) for i in range(2)]
        x_in = [sb1(f"x_in{i}", [P, TPB, D], F32) for i in range(NX)]
        wo = pair("wo", [P, KT, D])
        stats = [sb1(f"stats{i}", [P, TPB, 6], F32) for i in range(2)]
        mv = [sb1(f"mv{i}", [P, TPB, 2], F32) for i in range(2)]
        veps = [sb1(f"veps{i}", [P, TPB], F32) for i in range(2)]
        shift = [sb1(f"shift{i}", [P, TPB], F32) for i in range(2)]
        rstd = [sb1(f"rstd{i}", [P, TPB], F32) for i in range(2)]
        rsum = sb1("rsum", [P, TPB, H], F32)
        o_sb = sb1("o_sb", [P, TPB, D], F32)
        oTn = pair("oTn", [P, KT, S])
        until_mixed = used[0]
        wsg = pair("wsg", [P, KT, 2 * SI + E])
        ws2 = pair("ws2", [IC, NC_S, D])
        x1 = [sb1(f"x1_{i}", [P, TPB, D], F32) for i in range(2)]
        x2T = [pair(f"x2T{i}", [P, KT, S]) for i in range(2)]
        gate_t, gate_u, hid = ([sb1(f"{x}{f}", [P, I], F32) for f in range(2)] for x in ("gate_t", "gate_u", "hid"))
        hidT = [pair(f"hidT{i}", [IC, NC_S, P]) for i in range(TPB)]
        until_shared = used[0]
        xn2 = [sb1(f"xn2_{i}", [P, TPB, ROW], F32) for i in range(NXN)]
        base = [sb1(f"base{i}", [P, TPB, D], F32) for i in range(2)]
        lg = [sb1(f"lg{i}", [P, TPB, E], F32) for i in range(2)]
        rows_of = [sb1(f"rows_of{i}", [P, TPB, TOPK], I32) for i in range(2)]
        lmax = sb1("lmax", [P, TPB], F32)
        lsum = sb1("lsum", [P, TPB], F32)
        score = sb1("score", [P, TPB, E], F32)
        g8 = sb1("g8", [P, TPB, 8], F32)
        gtop = sb1("gtop", [P, TPB, 8], F32)
        gidx = sb1("gidx", [P, TPB, 8], U32)
        gidf = sb1("gidf", [P, TPB, TOPG], F32)
        geq = sb1("geq", [P, TPB, TOPG, G], F32)
        gsel = sb1("gsel", [P, TPB, G], F32)
        masked = sb1("masked", [P, TPB, E], F32)
        etop = sb1("etop", [P, TPB, 8], F32)
        eidx = sb1("eidx", [P, TPB, 8], U32)
        eidf = sb1("eidf", [P, TPB, TOPK], F32)
        onehot = sb1("onehot", [P, TPB, TOPK, E], F32)
        picks = sb1("picks", [P, TPB, E], BF16)
        place = sb1("place", [P, TPB, E], F32)
        placed = sb1("placed", [P, TPB, TOPK, E], F32)

        part1.close()
        part2 = ExitStack()

        def sb2(name, shape, dt):
            return sb(name, shape, dt, part2)

        LOADS = 4
        NXB, NYB, NST, NW = 5, 3, 4, 6
        st = [sb2(f"st{i}", [P, WE], F32) for i in range(NST)]
        wexp = sb2("wexp", [P, E * 2 * WE], F32R)

        d_const = done("d_const")
        d_zero = done("d_zero")
        d_w = [done(f"d_w{i}") for i in range(NST)]
        d_stage = done("d_stage")
        d_x = [done(f"d_x{i}") for i in range(NX)]
        d_scr = done("d_scr")
        d_stack = [[done(f"d_stack{i}_{half}") for half in range(2)] for i in range(2)]
        d_nmax = [[done(f"d_nmax{i}_{half}") for half in range(2)] for i in range(2)]
        d_base = [done(f"d_base{i}") for i in range(2)]
        d_rows = [done(f"d_rows{i}") for i in range(NXN)]

        def load_x(b):
            return sp.dma(lambda e: e.dma_start(x_in[b % NX][:], a["x"][b].rearrange("(i p) d -> p i d", p=P)),
                          d_x[b % NX], [x_read[b - NX] if b >= NX else None])

        def zero_sums():
            for i in range(NACC):
                first = T if i == 0 else 0
                rows = acc_scr[i][first:T + P].rearrange("(n p) d -> p n d", p=P)
                n = (T + P - first) // P
                sp.dma(lambda e, rows=rows, n=n: e.dma_start(
                    rows, zero[:, 0:D].rearrange("p (o d) -> p o d", o=1).to_broadcast([P, n, D])), d_zero, [z_zero])

        x_read, x_ready = {}, {}
        x_ready[0] = load_x(0)

        z = pool.add(lambda e: e.memset(zero[:], 0.0))
        z_zero = pool.add(lambda e: e.iota(zero[:, TOKEN:TOKEN + 1].bitcast(I32), pattern=[[1, 1]], base=T,
                                           channel_multiplier=1), [z])
        pool.add(lambda e: e.iota(blk[:], pattern=[[1, NBLK]], base=0, channel_multiplier=0,
                                  allow_small_or_imprecise_dtypes=True))
        pool.add(lambda e: e.memset(ident[:], 0.0))
        z = pool.add(lambda e: e.memset(half_pow[:], -0.5))
        c_ident = pool.add(lambda e: e.affine_select(out=ident[:], in_=ident[:], compare_op=ALU.not_equal, fill=1.0,
                                                     base=0, pattern=[[-1, P]], channel_multiplier=1), [z])
        c_identb = dve.add(lambda e: e.tensor_copy(ident_b[:], ident[:]), [c_ident])
        pool.add(lambda e: e.memset(mask_b[:], 0.0))
        pool.add(lambda e: e.memset(ones_b[:], 1.0))
        pool.add(lambda e: e.memset(chosen[:], 0.0))
        pool.add(lambda e: e.memset(upto_b[:], 1.0))
        z = pool.add(lambda e: e.memset(before_b[:], 1.0))
        pool.add(lambda e: e.affine_select(out=mask_b[:], in_=mask_b[:], compare_op=ALU.is_ge, fill=NEG,
                                           base=0, pattern=[[0, 2], [-1, P]], channel_multiplier=1), [z])
        pool.add(lambda e: e.affine_select(out=upto_b[:], in_=upto_b[:], compare_op=ALU.is_ge, fill=0.0,
                                           base=0, pattern=[[1, E]], channel_multiplier=-1), [z])
        c_masks = pool.add(lambda e: e.affine_select(out=before_b[:], in_=before_b[:], compare_op=ALU.is_gt, fill=0.0,
                                                     base=0, pattern=[[1, P]], channel_multiplier=-1), [z])
        pool.add(lambda e: e.iota(iota_e[:], pattern=[[1, E]], base=0, channel_multiplier=0,
                                  allow_small_or_imprecise_dtypes=True))
        c_iota = pool.add(lambda e: e.iota(region[:], pattern=[[CAP, E]], base=0, channel_multiplier=0,
                                           allow_small_or_imprecise_dtypes=True))
        pool.add(lambda e: e.memset(g8[:], -1.0))
        for v in xn2:
            z = pool.add(lambda e, v=v: e.memset(v[:, :, TOKEN:ROW], 0.0))

        def split_hi(hi, src, waits):
            return act.add(lambda e: e.activation(hi, src, ACT.Copy), waits)

        def split_lo(lo, hi, src, waits):
            return dve.add(lambda e: e.tensor_tensor(lo, src, hi.bitcast(F32), ALU.subtract), waits)

        def split(dst, src, waits_hi, waits_lo=()):
            hi, lo = dst
            t_hi = split_hi(hi, src, waits_hi)
            return t_hi, split_lo(lo, hi, src, [t_hi, *waits_lo])

        ready = {}

        def load_weights(name, dst, rows, waits=()):
            k, n = dst[0].shape[1], dst[0].shape[2]
            view = wstage[0:rows, 0:k * n].rearrange("p (k n) -> p k n", k=k)
            t = sp.dma(lambda e: e.dma_start(view, a[name].rearrange("(k p) n -> p k n", p=rows)), d_stage, waits)
            for _ in range(4):
                yield
            hi = split_hi(dst[0][:], view, [t])
            yield
            ready[name] = split_lo(dst[1][:], dst[0][:], view, [hi])

        def setup():
            for v in vhat:
                z = pool.add(lambda e, v=v: e.memset(v[:], 0.0))
            for v in vhat:
                ready["vhat"] = pool.add(lambda e, v=v: e.memset(v[:, :, :, HD:HD + 1], 1.0), [z])
            ready["kst"] = pool.add(lambda e: e.memset(kst[:].bitcast(F32), 1.0))
            yield
            while "wqkv" not in ready:
                yield
            yield from load_weights("wo", wo, P, [ready["wqkv"]])
            yield from load_weights("wsg", wsg, P, [ready["wo"]])
            yield from load_weights("ws2", ws2, IC, [ready["wsg"]])

        x_ready[1] = load_x(1)
        sp.dma(lambda e: e.dma_start(cos_t[:], a["rope_cos"]), d_const)
        c_rope = sp.dma(lambda e: e.dma_start(sin_t[:], a["rope_sin"]), d_const)
        passes = ((0, 0), (0, 1), (1, 0))

        def product(region, stationary, moving, contraction, waits, first_starts=True):
            n = 3 * contraction
            for j in range(n):
                k, (s, m) = j // 3, passes[j % 3]
                t = pe.add(lambda e, k=k, s=s, m=m, j=j: e.matmul(
                    region, stationary(s, k), moving(m, k), start=(j == 0 and first_starts), stop=(j == n - 1),
                    skip_group_check=True), waits if j == 0 else (), signal=(j == n - 1))
            return t

        def norm(x_tile, x_tok, dst, dst_free, which):
            st, m, v, r = stats[which], mv[which], veps[which], rstd[which]
            for i in range(TPB):
                t = dve.add(lambda e, i=i: e.bn_stats(st[:, i, :], x_tile[:, i, :]), [x_tok])
            yield
            for i in range(TPB):
                t2 = dve.add(lambda e, i=i: e.bn_aggr(m[:, i, :], st[:, i, :]), [t])
            yield
            t = dve.add(lambda e: e.tensor_scalar(v[:], m[:, :, 1], EPS, None, ALU.add), [t2])
            yield
            t = pool.add(lambda e: e.tensor_tensor(r[:], v[:], half_pow[:], ALU.pow), [t])
            yield
            yield
            s = shift[which]
            t = dve.add(lambda e: e.scalar_tensor_tensor(out=s[:], in0=m[:, :, 0], scalar=-1.0, in1=r[:],
                                                         op0=ALU.mult, op1=ALU.mult), [t, *dst_free])
            yield
            for i in range(TPB):
                t2 = act.add(lambda e, i=i: e.activation(dst[:, i, 0:D], x_tile[:, i, :], ACT.Identity,
                                                         bias=s[:, i:i + 1], scale=r[:, i:i + 1]), [t, x_tok, *dst_free])
            yield
            return t2

        def turned(src, src_tok, dst, dst_free):
            n = yield from take(SHARED)
            for k in range(KT):
                for i in range(TPB):
                    t = pe.add(lambda e, k=k, i=i: e.transpose(
                        bank[n][:, k * S + i * P:k * S + (i + 1) * P], src[:, i, k * P:(k + 1) * P], ident[:]),
                        [src_tok, c_ident, *free[n]], signal=(k == KT - 1 and i == TPB - 1))
            yield
            view = bank[n][:, 0:KT * S].rearrange("p (k s) -> p k s", k=KT)
            hi = split_hi(dst[0][:], view, [t, *dst_free])
            yield
            lo = split_lo(dst[1][:], dst[0][:], view, [hi])
            give(SHARED, n, lo)
            yield
            return t, lo

        def exact_sum(e, dst, src):
            with nc.allow_low_precision(reason="sums of whole numbers that the type holds exactly"):
                return e.tensor_reduce(dst, src, AX.X, ALU.add)

        q = {}

        def past(name, b, *more):
            return q[(name, b, *more)] if b >= 0 else None

        def project(b):
            tok = yield from norm(x_in[b % NX], x_ready[b], xn, [past("xn_read", b - 1)], 0)
            q["xn_read", b], xT_ready = yield from turned(xn, tok, xT, [past("xT_read", b - 1)])
            for qk in range(2):
                n = yield from take(SHARED)
                for two in range(2):
                    col = (2 * qk + two) * P
                    t = product(bank[n][:, two * S:(two + 1) * S],
                                lambda s, k, col=col: wqkv[s][:, k, col:col + P],
                                lambda m, k: xT[m][:, k, :], KT, [xT_ready, ready["wqkv"], *free[n]])
                yield
                ev, od = bank[n][:, 0:S], bank[n][:, S:2 * S]
                w = [past("roped_read", b - 1)]
                t1 = dve.add(lambda e, ev=ev: e.tensor_tensor(rope_a[:], ev, cos_t[:], ALU.mult),
                             [t, c_rope, q.get("rope_sub")])
                t2 = dve.add(lambda e, od=od: e.tensor_tensor(rope_b[:], od, sin_t[:], ALU.mult))
                yield
                t3 = pool.add(lambda e, qk=qk: e.tensor_tensor(roped[:, 0, qk, :], rope_a[:], rope_b[:], ALU.subtract),
                              [t2, *w])
                q["rope_sub"] = t3
                t4 = dve.add(lambda e, ev=ev: e.tensor_tensor(rope_c[:], ev, sin_t[:], ALU.mult), [q.get("rope_add")])
                t5 = dve.add(lambda e, od=od: e.tensor_tensor(rope_d[:], od, cos_t[:], ALU.mult))
                give(SHARED, n, t5)
                yield
                t6 = pool.add(lambda e, qk=qk: e.tensor_tensor(roped[:, 1, qk, :], rope_c[:], rope_d[:], ALU.add),
                             [t5, *w])
                q["rope_add"] = t6
            n = yield from take(SHARED)
            for i in range(TPB):
                t = product(bank[n][:, i * D:(i + 1) * D],
                            lambda s, k, i=i: xT[s][:, k, i * P:(i + 1) * P],
                            lambda m, k: wqkv[m][:, k, 2 * D:3 * D], KT, free[n])
            q["xT_read", b] = t
            yield
            vt = act.add(lambda e: e.activation(vhat[b % NV][:, :, :, 0:HD],
                                                bank[n][:, 0:TPB * D].rearrange("p (i h d) -> p i h d", i=TPB, h=H),
                                                ACT.Copy), [t, ready["vhat"], past("pv", b - NV)])
            q["v", b] = vt
            give(SHARED, n, vt)
            hi = split_hi(ropeds[0][:], roped[:], [t3, t6, past("scr_done", b - 1)])
            yield
            yield
            lo = split_lo(ropeds[1][:], ropeds[0][:], roped[:], [hi, past("scr_done", b - 1)])
            q["roped_read", b] = lo
            for s, t in ((0, hi), (1, lo)):
                for r in range(2):
                    w = sp.dma(lambda e, s=s, r=r: e.dma_start(qk_scr[b, :, s, r].rearrange("q w t -> w q t"),
                                                              ropeds[s][:, r, :, :].bitcast(F32)), d_scr, [t])
            q["scr_done", b] = w
            o = 64 * (b % 2)
            back = [qk_scr[b, j].rearrange("s r (p h) t -> (s r p) h t", h=H) for j in range(2)]
            for half, hs in enumerate(HALVES):
                ws = [w, past("attended", b - 2, half), ready["kst"]]
                d = d_stack[b % 2][half]
                sp.dma(lambda e, hs=hs: e.dma_start(qst[o:o + SLOT, hs, :].bitcast(F32), back[0][0:SLOT, hs]), d, ws)
                sp.dma(lambda e, hs=hs: e.dma_start(qst[o + SLOT:o + KB, hs, :].bitcast(F32), back[0][:, hs]), d)
                sp.dma(lambda e, hs=hs: e.dma_start(kst[o:o + 2 * SLOT, hs, :].bitcast(F32), back[1][:, hs]), d)
                q["stack", b, half] = sp.dma(lambda e, hs=hs: e.dma_start(
                    kst[o + 2 * SLOT:o + KB, hs, :].bitcast(F32), back[1][0:SLOT, hs]), d)

        def row_maxima(b):
            o = 64 * (b % 2)
            for half, hs in enumerate(HALVES):
                for h in range(hs.start, hs.stop, 2):
                    for i in range(TPB):
                        n = yield from take(SHARED)
                        view = bank[n][:].rearrange("p (h k) -> p h k", h=2)
                        for j in range(2):
                            pe.add(lambda e, j=j, h=h, i=i, n=n: e.matmul(
                                bank[n][:, j * S:(j + 1) * S], qst[o:o + KB, h + j, i * P:(i + 1) * P],
                                kst[o:o + KB, h + j, :], start=(j == 0), stop=False, skip_group_check=True),
                                [q["stack", b, half], *free[n]] if j == 0 else (), signal=False)
                        t = pe.add(lambda e, i=i, view=view: e.matmul(
                            view[:, :, i * P:(i + 1) * P], ident_b[:], mask_b[:], start=False, stop=True,
                            skip_group_check=True), [c_identb, c_masks])
                        yield
                        tm = dve.add(lambda e, i=i, h=h, view=view: e.tensor_reduce(
                            row_max[:, i, h:h + 2], view[:, :, 0:(i + 1) * P], AX.X, ALU.max),
                            [t, past("max_turned", b - 1, half)])
                        give(SHARED, n, tm)
                yield
                n = yield from take(SHARED)
                for i in range(TPB):
                    t = pe.add(lambda e, i=i, hs=hs, n=n: e.transpose(
                        bank[n][0:H // 2, i * P:(i + 1) * P], row_max[:, i, hs], ident[:]),
                        [tm, *free[n]], signal=(i == TPB - 1))
                q["max_turned", b, half] = t
                yield
                hi = act.add(lambda e, n=n, half=half: e.activation(nmax[:, half, 0, :], bank[n][0:H // 2, 0:S],
                                                                    ACT.Copy, scale=-1.0),
                             [t, past("nmax_done", b - 1, half)])
                yield
                lo = dve.add(lambda e, n=n, half=half: e.scalar_tensor_tensor(
                    out=nmax[:, half, 1, :], in0=bank[n][0:H // 2, 0:S], scalar=-1.0,
                    in1=nmax[:, half, 0, :].bitcast(F32), op0=ALU.mult, op1=ALU.subtract), [hi])
                give(SHARED, n, lo)
                for j in range(2):
                    t = sp.dma(lambda e, j=j, half=half, hs=hs: e.dma_start(
                        qst[o + KB + j:o + KB + j + 1, hs, :].bitcast(F32), nmax[:, half, j, :].bitcast(F32)),
                        d_nmax[b % 2][half], [lo])
                q["nmax_done", b, half] = t

        def attend(b):
            o = 64 * (b % 2)
            pending, copy_out = None, None
            for g in range(H // 4):
                pt = probs[(4 * b + g) % NPT]
                for u in range(2):
                    exps = []
                    for kt in range(2):
                        n = yield from take(SCORES)
                        view = bank[n][:].rearrange("p (h q) -> p h q", h=2)
                        for j in range(2):
                            h = 4 * g + 2 * u + j
                            t = pe.add(lambda e, j=j, h=h, kt=kt, n=n: e.matmul(
                                bank[n][:, j * S:(j + 1) * S], kst[o:o + KA, h, kt * P:(kt + 1) * P],
                                qst[o:o + KA, h, :], start=(j == 0), stop=(j == 1), skip_group_check=True),
                                [q["nmax_done", b, g // 2], q["stack", b, g // 2], *free[n]], signal=(j == 1))
                        dst = (pt[:, 0:3:2, 2 * u:2 * u + 2, :].rearrange("p c h q -> p h c q") if kt == 0
                               else pt[:, 1, 2 * u:2 * u + 2, :])
                        src = (view.rearrange("p h (c q) -> p h c q", c=2) if kt == 0 else view[:, :, P:])
                        exps.append((n, dst, src, t))
                    yield
                    for n, dst, src, t in exps:
                        te = act.add(lambda e, dst=dst, src=src: e.activation(dst, src, ACT.Exp, scale=0.25),
                                     [t, past("pv_read", 4 * b + g - NPT)])
                        give(SCORES, n, te)
                    if u == 0 and pending:
                        pending()
                    if u == 1 and copy_out:
                        copy_out()
                    yield
                q["attended", b, g // 2] = t
                diag = pt[:, 0:2, :, :].rearrange("p c h q -> p (c h q)")
                ts = pool.add(lambda e, diag=diag: e.affine_select(
                    out=diag, in_=diag, compare_op=ALU.is_ge, fill=0.0, base=0,
                    pattern=[[0, 8], [1, P]], channel_multiplier=-1), [te])

                def pending(g=g, pt=pt, ts=ts):
                    n, = OUT
                    for kt in range(2):
                        for j in range(4):
                            mov = pt[:, 0:3:2, j, :] if kt == 0 else pt[:, 1, j, :]
                            t = pe.add(lambda e, j=j, kt=kt, mov=mov: e.matmul(
                                bank[n][32 * j:32 * j + VW, kt * P:S], vhat[b % NV][:, kt, 4 * g + j, :], mov,
                                start=(kt == 0), stop=(kt == 1), skip_group_check=True),
                                [ts, q["v", b], *free[n]], signal=(kt == 1 and j == 3))
                    q["pv_read", 4 * b + g] = q["pv", b] = t

                def copy_out(g=g):
                    n, = OUT
                    tc = act.add(lambda e: e.activation(oT[b % 2][:, g, :], bank[n][:, 0:S], ACT.Copy),
                                 [q["pv_read", 4 * b + g], past("oT_read", b - 2)])
                    free[n] = [tc]
                    q["oT", b] = tc
            yield
            pending()
            yield
            copy_out()

        def mix(b):
            x2 = xn2[b % NXN]
            for i in range(TPB):
                n = yield from take(SHARED)
                for g in range(4):
                    t = pe.add(lambda e, g=g, i=i, n=n: e.transpose(
                        bank[n][:, g * P:(g + 1) * P], oT[b % 2][:, g, i * P:(i + 1) * P], ident[:]),
                        [q["oT", b], *free[n]], signal=(g == 3))
                yield
                heads = bank[n][:].rearrange("p (h w) -> p h w", w=VW)
                tr = dve.add(lambda e, i=i, heads=heads: e.reciprocal(rsum[:, i, :], heads[:, :, HD]), [t])
                to = dve.add(lambda e, i=i, heads=heads: e.tensor_tensor(
                    o_sb[:, i, :].rearrange("p (h d) -> p h d", h=H), heads[:, :, 0:HD],
                    rsum[:, i, :].rearrange("p (h o) -> p h o", o=1).to_broadcast([P, H, HD]), ALU.mult),
                    [tr, past("o_read", b - 1)])
                give(SHARED, n, to)
            yield
            q["oT_read", b] = t
            q["o_read", b], oTn_ready = yield from turned(o_sb, to, oTn, [past("oTn_read", b - 1)])
            n = yield from take(SHARED)
            for i in range(TPB):
                t = product(bank[n][:, i * D:(i + 1) * D], lambda s, k, i=i: oTn[s][:, k, i * P:(i + 1) * P],
                            lambda m, k: wo[m][:, k, :], KT, [oTn_ready, ready["wo"], *free[n]])
            q["oTn_read", b] = t
            yield
            t1 = dve.add(lambda e, n=n: e.tensor_tensor(x1[b % 2][:].rearrange("p i d -> p (i d)"),
                                                        bank[n][:, 0:TPB * D],
                                                        x_in[b % NX][:].rearrange("p i d -> p (i d)"), ALU.add),
                         [t, past("x1_read", b - 2)])
            give(SHARED, n, t1)
            x_read[b] = t1
            yield
            tn = yield from norm(x1[b % 2], t1, x2, [past("rows_done", b - NXN), past("x2_turned", b - NXN)], 1)
            q["x2_turned", b], q["x2T", b] = yield from turned(x2, tn, x2T[b % 2], [past("x2T_read", b - 2)])
            q["x2", b] = tn

        def shared_tile(b, i):
            for f in range(2):
                n = yield from take(SHARED)
                c0, width = ((0, 2 * I + E), (2 * I + E, 2 * I))[f]
                ta = product(bank[n][:, 0:width], lambda s, k: x2T[b % 2][s][:, k, i * P:(i + 1) * P],
                             lambda m, k, c0=c0, width=width: wsg[m][:, k, c0:c0 + width], KT,
                             [q["x2T", b], ready["wsg"], *free[n]])
                q["x2T_read", b] = ta
                yield
                tt = act.add(lambda e, n=n: e.activation(gate_t[i][:], bank[n][:, 0:I], ACT.Tanh, scale=0.5),
                             [ta, q.get(("gate_read", i))])
                if f == 0:
                    tt = act.add(lambda e, n=n: e.activation(lg[b % 2][:, i, :], bank[n][:, 2 * I:2 * I + E],
                                                             ACT.Copy), [past("lg_read", b - 2)])
                    q["lg", b, i] = tt
                yield
                tu = dve.add(lambda e, n=n: e.scalar_tensor_tensor(
                    out=gate_u[i][:], in0=gate_t[i][:], scalar=1.0, in1=bank[n][:, 0:I], op0=ALU.add,
                    op1=ALU.mult), [tt])
                q["gate_read", i] = tu
                th = dve.add(lambda e, n=n: e.scalar_tensor_tensor(
                    out=hid[i][:], in0=gate_u[i][:], scalar=0.5, in1=bank[n][:, I:2 * I], op0=ALU.mult,
                    op1=ALU.mult), [tu, q.get(("hid_read", i))])
                give(SHARED, n, th)
                yield
                n = yield from take(SHARED)
                for c in range(2):
                    t = pe.add(lambda e, c=c, n=n: e.transpose(bank[n][0:IC, c * P:(c + 1) * P],
                                                               hid[i][:, c * IC:(c + 1) * IC], ident[:]),
                               [th, *free[n]], signal=(c == 1))
                q["hid_read", i] = t
                yield
                view = bank[n][0:IC, 0:2 * P].rearrange("p (c t) -> p c t", c=2)
                dst = [u[:, 2 * f:2 * f + 2, :] for u in hidT[i]]
                hi = split_hi(dst[0], view, [t, q.get(("hidT_read", i))])
                yield
                lo = split_lo(dst[1], dst[0], view, [hi])
                give(SHARED, n, lo)
            yield
            n = yield from take(SHARED)
            t = product(bank[n][:, 0:D], lambda s, k: hidT[i][s][:, k, :], lambda m, k: ws2[m][:, k, :], NC_S,
                        [lo, ready["ws2"], *free[n]])
            q["hidT_read", i] = t
            yield
            tbase = dve.add(lambda e, n=n: e.tensor_tensor(base[b % 2][:, i, :], bank[n][:, 0:D], x1[b % 2][:, i, :],
                                                           ALU.add), [t, past("base_done", b - 2)])
            give(SHARED, n, tbase)
            q["x1_read", b] = tbase

        def shared(b):
            first, second = shared_tile(b, 0), shared_tile(b, 1)
            for _ in range(3):
                next(first)
                yield
            live = [second, first]
            while live:
                for g in list(live):
                    try:
                        next(g)
                    except StopIteration:
                        live.remove(g)
                yield
            q["base_done", b] = sp.dma(lambda e: e.dma_start(
                acc_scr[0][b * S:(b + 1) * S].rearrange("(i p) d -> p i d", p=P), base[b % 2][:]), d_base[b % 2],
                [q["x1_read", b]])

        def route(b):
            x2, logits = xn2[b % NXN], lg[b % 2]

            def v(build, *waits):
                return dve.add(build, waits)

            def bc(ap, shape):
                return ap.to_broadcast(shape)
            t = v(lambda e: e.tensor_reduce(lmax[:], logits[:], AX.X, ALU.max), q["lg", b, 0], q["lg", b, 1])
            yield
            t = v(lambda e: e.tensor_tensor(logits[:], logits[:],
                                            bc(lmax[:].rearrange("p (i o) -> p i o", o=1), [P, TPB, E]),
                                            ALU.subtract), t)
            yield
            t = act.add(lambda e: e.activation(logits[:], logits[:], ACT.Exp), [t])
            tt = pool.add(lambda e: e.iota(x2[:, :, TOKEN:TOKEN + 1].bitcast(I32), pattern=[[P, TPB], [1, 1]],
                                           base=b * S, channel_multiplier=1), [q["x2", b]])
            yield
            t = v(lambda e: e.tensor_reduce(lsum[:], logits[:], AX.X, ALU.add), t)
            yield
            t = v(lambda e: e.reciprocal(lsum[:], lsum[:]), t)
            yield
            t = v(lambda e: e.tensor_tensor(score[:], logits[:], bc(lsum[:].rearrange("p (i o) -> p i o", o=1),
                                                                   [P, TPB, E]), ALU.mult), t)
            q["lg_read", b] = t
            yield
            by_group = score[:].rearrange("p i (g m) -> p i g m", g=G)
            t = v(lambda e: e.tensor_reduce(g8[:, :, 0:G], by_group, AX.X, ALU.max), t, c_iota)
            yield
            for i in range(TPB):
                t = v(lambda e, i=i: e.max(gtop[:, i, :], g8[:, i, :]), t)
            yield
            for i in range(TPB):
                t = v(lambda e, i=i: e.max_index(gidx[:, i, :], gtop[:, i, :], g8[:, i, :]), t)
            yield
            t = v(lambda e: e.tensor_copy(gidf[:], gidx[:, :, 0:TOPG]), t)
            yield
            full = [P, TPB, TOPG, G]
            t = v(lambda e: e.tensor_tensor(
                geq[:], bc(iota_e[:, 0:G].rearrange("p (i k g) -> p i k g", i=1, k=1), full),
                bc(gidf[:].rearrange("p i (k o) -> p i k o", o=1), full), ALU.is_equal), t)
            yield
            t = v(lambda e: e.tensor_tensor(gsel[:], geq[:, :, 0, :], geq[:, :, 1, :], ALU.add), t)
            yield
            selb = bc(gsel[:].rearrange("p i (g o) -> p i g o", o=1), [P, TPB, G, E // G])
            mview = masked[:].rearrange("p i (g m) -> p i g m", g=G)
            t = v(lambda e: e.tensor_tensor(mview, by_group, selb, ALU.mult), t)
            yield
            t = v(lambda e: e.scalar_tensor_tensor(out=mview, in0=selb, scalar=-1.0, in1=mview, op0=ALU.add,
                                                   op1=ALU.add), t)
            yield
            for i in range(TPB):
                t = v(lambda e, i=i: e.max(etop[:, i, :], masked[:, i, :]), t)
            yield
            for i in range(TPB):
                t = v(lambda e, i=i: e.max_index(eidx[:, i, :], etop[:, i, :], masked[:, i, :]), t)
            yield
            t = v(lambda e: e.tensor_copy(eidf[:], eidx[:, :, 0:TOPK]), t)
            yield
            full2 = [P, TPB, TOPK, E]
            t = v(lambda e: e.tensor_tensor(
                onehot[:], bc(iota_e[:].rearrange("p (i k e) -> p i k e", i=1, k=1), full2),
                bc(eidf[:].rearrange("p i (k o) -> p i k o", o=1), full2), ALU.is_equal), t)
            yield
            t = v(lambda e: exact_sum(e, picks[:], onehot[:].rearrange("p i k e -> p i e k")), t,
                  past("ranked", b - 1), past("chosen", b - 1))
            yield
            tw = v(lambda e: e.tensor_tensor(x2[:, :, D:D + E], score[:], picks[:], ALU.mult), t)
            n = yield from take(SHARED)
            pe.add(lambda e: e.matmul(bank[n][:, 0:E], before_b[:], picks[:, 0, :], start=True, stop=False,
                                      skip_group_check=True), [t, past("chosen", b - 1), c_masks, *free[n]],
                   signal=False)
            pe.add(lambda e: e.matmul(bank[n][:, 0:E], ones_b[:], chosen[:], start=False, stop=True,
                                      skip_group_check=True), (), signal=False)
            pe.add(lambda e: e.matmul(bank[n][:, E:2 * E], before_b[:], picks[:, 1, :], start=False, stop=False,
                                      skip_group_check=True), (), signal=False)
            pe.add(lambda e: e.matmul(bank[n][:, E:2 * E], ones_b[:], picks[:, 0, :], start=False, stop=False,
                                      skip_group_check=True), (), signal=False)
            t2 = pe.add(lambda e: e.matmul(bank[n][:, E:2 * E], ones_b[:], chosen[:], start=False, stop=True,
                                           skip_group_check=True))
            q["ranked", b] = t2
            t = v(lambda e: e.tensor_tensor(place[:], bank[n][:, 0:TPB * E].rearrange("p (i e) -> p i e", i=TPB),
                                            bc(region[:].rearrange("p (i e) -> p i e", i=1), [P, TPB, E]), ALU.add), t2)
            give(SHARED, n, t)
            t3 = pool.add(lambda e: e.tensor_tensor(chosen[:], chosen[:], picks[:, 0, :], ALU.add), [t2])
            q["chosen", b] = pool.add(lambda e: e.tensor_tensor(chosen[:], chosen[:], picks[:, 1, :], ALU.add), [t3])
            yield
            t = v(lambda e: e.tensor_tensor(placed[:], onehot[:], bc(place[:].rearrange("p i (k e) -> p i k e", k=1),
                                                                     full2), ALU.mult), t)
            yield
            t = v(lambda e: exact_sum(e, rows_of[b % 2][:], placed[:]), t, past("rows_done", b - 2))
            yield
            for i in range(TPB):
                for k in range(TOPK):
                    w = pool.dma(lambda e, i=i, k=k: e.indirect_dma_start(
                        rows_scr[:, :], bass.IndirectOffsetOnAxis(ap=rows_of[b % 2][:, i, k:k + 1].bitcast(U32),
                                                                  axis=0), x2[:, i, :], None), d_rows[b % NXN],
                        [t, tt, tw])
                    if k % 2:
                        yield
            q["rows_done", b] = w

        finished = set()
        w_free = [None] * NST
        loaded = {}

        def load_expert(x, over):
            i = x % NST
            loaded[x] = sp.dma(lambda e: e.dma_start(st[i][:], a["wexp"][x]), d_w[i], [w_free[i], *over])

        def split_expert(x, over):
            i = x % NST
            hi, lo = (wexp[:, (2 * x + m) * WE:(2 * x + m + 1) * WE] for m in range(2))
            th = split_hi(hi, st[i][:], [loaded[x], *over])
            yield
            w_free[i] = split_lo(lo, hi, st[i][:], [th])

        def over_now():
            return ([(u.sem, u.count) for u in (pe, act, dve, pool)]
                    + [(u.sem, u.count) for u in (d_const, d_stage, d_scr, *d_x, *sum(d_stack, []), *sum(d_nmax, []))])

        over_attend, over_mix, over_shared = (min(E, (until - NST * WE * 4) // (2 * WE * 4))
                                              for until in (until_attended, until_mixed, until_shared))
        assert over_shared == E

        def expert_weights():
            x = 0
            for stage, last in ((attend, over_attend), (mix, over_mix)):
                while stage not in finished:
                    yield
                over = over_now()
                for x in range(x, last):
                    for y in range(x, min(x + 2, last)):
                        if y not in loaded:
                            load_expert(y, over)
                    yield
                    yield
                    yield
                    yield from split_expert(x, over)
                x = last
            while shared not in finished:
                yield
            for x in range(x, min(x + NST, E)):
                load_expert(x, over_now())

        def last_batch(stage):
            yield from stage(B - 1)
            finished.add(stage)

        def loads(b):
            x_ready[b] = load_x(b)
            if b == 3:
                zero_sums()
            yield

        plan = (((2.103, 2.799), 18, attend),
                ((1.103, 2.032), 23, row_maxima),
                ((0, 0.673), 18, project),
                ((2.822, 3.834), 17, mix),
                ((4.092, 4.97), 16, shared),
                ((5.023, 5.919), 26, route),
                ((-1, -0.99), 1, loads))
        runs = [(b + start, b + end, steps, last_batch(stage) if b == B - 1 else stage(b))
                for b in range(B) for (start, end), steps, stage in plan if stage is not loads or b >= 2]
        runs += [(0, 0.3, 10, load_weights("wqkv", wqkv, P)), (0.1, 3.5, 19, setup()),
                 (B - 1 + 2.799, B - 1 + 5.919, 60, expert_weights())]
        merge(runs)

        over = [(u.sem, u.count) for u in (pe, act, dve, pool)]
        over += [(u.sem, u.count) for u in (d_const, d_stage, d_scr, *d_x, *sum(d_stack, []), *sum(d_nmax, []), *d_base, *d_rows)]
        xb = [sb2(f"xb{i}", [P, ROW], F32) for i in range(NXB)]
        xbT = [pair(f"xbT{i}", [P, KT, P], part2) for i in range(2)]
        silu = sb2("silu", [P, I], F32)
        up = [sb2(f"up{i}", [P, I], F32) for i in range(2)]
        upT = [pair(f"upT{i}", [IC, NC_E, P], part2) for i in range(2)]
        yb = [sb2(f"yb{i}", [P, D], F32) for i in range(NYB)]
        picked = sb2("picked", [P, E], F32)
        weight = [sb2(f"weight{i}", [P, 1], F32) for i in range(NW)]
        token = [sb2(f"token{i}", [P, 1], I32) for i in range(NW)]
        d_tail = done("d_tail")
        d_xb = [done(f"d_xb{i}") for i in range(NXB)]
        d_add = [done(f"d_add{i}") for i in range(NACC)]

        cb, eb = 0, 1
        pe.add(lambda e: e.matmul(bank[cb][:, 0:E], ones_b[:], chosen[:], start=True, stop=True,
                                  skip_group_check=True), [*free[cb], *free[eb], q["chosen", B - 1]])
        tc = pe.add(lambda e: e.matmul(bank[cb][0:E, P:2 * P], chosen[:], ones_b[:], start=True, stop=True,
                                       skip_group_check=True))
        def v(build, *waits):
            return dve.add(build, waits)

        t_tail = v(lambda e: e.tensor_tensor(tail[:], bank[cb][0:1, 0:E], region[0:1, :], ALU.add), tc)
        t = v(lambda e: e.tensor_scalar(nblk_i[:], bank[cb][0:E, P:2 * P], P / 2 - 0.5, 1.0 / P, ALU.add, ALU.mult))
        t_n = v(lambda e: e.tensor_copy(nblk[:], nblk_i[:]), t)
        pe.add(lambda e: e.matmul(bank[cb][0:E, E:E + 1], upto_b[:], nblk[:, 0:1], start=True, stop=True,
                                  skip_group_check=True), [t_n])
        te = pe.add(lambda e: e.matmul(bank[cb][:, E + 1:E + 2], nblk[:], ones_b[0:E, 0:1], start=True, stop=True,
                                       skip_group_check=True))
        t1 = v(lambda e: e.tensor_copy(ends[:], bank[cb][0:E, E:E + 1]), te)
        t = v(lambda e: e.tensor_copy(total[:], bank[cb][:, E + 1:E + 2]))
        t = v(lambda e: e.tensor_scalar(wrap[:], blk[:], total[:], total[:], ALU.is_ge, ALU.mult), t)
        t2 = v(lambda e: e.tensor_scalar(beyond[:], blk[:], total[:], None, ALU.is_ge), t)
        t = v(lambda e: e.tensor_tensor(blk[:], blk[:], wrap[:], ALU.subtract), t2)
        t = v(lambda e: e.tensor_scalar(past_b[:], blk[0:E, :], ends[:], None, ALU.is_ge), t)
        pe.add(lambda e: e.matmul(bank[eb][:, 0:NBLK], ones_b[0:E, :], past_b[:], start=True, stop=True,
                                  skip_group_check=True), [t])
        tp = pe.add(lambda e: e.matmul(bank[eb][:, NBLK:2 * NBLK], nblk[:], past_b[:], start=True, stop=True,
                                       skip_group_check=True))
        t = v(lambda e: e.tensor_copy(expert[:], bank[eb][:, 0:NBLK]), tp)
        t_off = v(lambda e: e.tensor_scalar(off_t[:], expert[:], float(2 * WE), None, ALU.mult), t)
        t = v(lambda e: e.tensor_tensor(row_f[:], blk[:], bank[eb][:, NBLK:2 * NBLK], ALU.subtract), t_off)
        t = v(lambda e: e.tensor_scalar(row_f[:], row_f[:], float(P), None, ALU.mult), t)
        t_row = v(lambda e: e.scalar_tensor_tensor(out=row_t[:], in0=expert[:], scalar=float(CAP), in1=row_f[:],
                                                   op0=ALU.mult, op1=ALU.add), t)
        t_picks = v(lambda e: e.scalar_tensor_tensor(out=picks_of[:], in0=beyond[:], scalar=float(E), in1=expert[:],
                                                     op0=ALU.mult, op1=ALU.add), t_row)
        free[cb] = free[eb] = [t_picks]

        def tails(queue, xs):
            def read(e):
                for x, reg in zip(xs, load_registers(e, "tail", tail[0:1, xs[0]:xs[-1] + 1])):
                    regs["tail", x] = e.snap(reg, min_val=0, max_val=E * CAP - P)
            queue.add(read, [t_tail], signal=False)
            for x in xs:
                queue.dma(lambda e, x=x: e.dma_start(rows_scr[bass.ds(regs["tail", x], P), :], zero[:]), d_tail,
                          [z_zero])

        def load_registers(e, name, table):
            out = [e.alloc_register(f"{name}{nc.get_next_instruction_name()}_{i}") for i in range(table.shape[-1])]
            e.load(out, table)
            return out

        regs = {}
        tails(sp, range(E))

        over = over_now()
        for x in range(over_mix, E):
            if x not in loaded:
                load_expert(x, over)
            for _ in split_expert(x, over):
                pass
        w_ready = w_free[(E - 1) % NST]

        r = {}

        def fetch(queue, key, table, top, waits):
            def build(e):
                regs[key] = e.value_load(table, min_val=0, max_val=top)
            queue.add(build, waits, signal=False)

        def load_rows(j):
            fetch(sp, ("x", j), row_t[0:1, j:j + 1], E * CAP - P, [t_row])
            r["x", j] = sp.dma(lambda e: e.dma_start(xb[j % NXB][:], rows_scr[bass.ds(regs["x", j], P), :]),
                               d_xb[j % NXB], [(d_tail.sem, d_tail.count), *((d.sem, d.count) for d in d_rows),
                                               *r.get(("x_read", j - NXB), ())])

        def turn_rows(j):
            n = (0, 1)[j % 2]
            x = xb[j % NXB]
            for k in range(KT):
                t = pe.add(lambda e, k=k: e.transpose(bank[n][:, k * P:(k + 1) * P], x[:, k * P:(k + 1) * P],
                                                      ident[:]), [r["x", j], *free[n]], signal=(k == KT - 1))
            t1 = dve.add(lambda e: e.tensor_copy(token[j % NW][:], x[:, TOKEN:TOKEN + 1].bitcast(I32)),
                         [r["x", j], r.get(("add", j - NW))])
            t2 = dve.add(lambda e: e.scalar_tensor_tensor(
                out=picked[:], in0=iota_e[:], scalar=picks_of[:, j:j + 1], in1=x[:, D:D + E], op0=ALU.is_equal,
                op1=ALU.mult), [t_picks, r.get(("weight", j - 1))])
            r["x_read", j] = [t, t2]
            hi, lo = split([u[:] for u in xbT[j % 2]], bank[n][:, 0:KT * P].rearrange("p (k t) -> p k t", k=KT),
                           [t, r.get(("xT_read", j - 2))])
            r["weight", j] = dve.add(lambda e: e.tensor_reduce(weight[j % NW][:], picked[:], AX.X, ALU.add),
                                     [t2, r.get(("y", j - NW))])
            free[n] = [lo]
            r["xT", j] = lo

        def hidden(j):
            n = (2, 3)[j % 2]
            t = product(bank[n][:, 0:SI], lambda s, k: xbT[j % 2][s][:, k, :],
                        lambda m, k: weights(j, m, k * SI, SI, P), KT,
                        [r["xT", j], w_ready, *free[n]])
            if j + 1 < NBLK and (j + 1) % LOADS == 0:
                fetch_weights(j + 1)
            r["xT_read", j] = t
            t = act.add(lambda e: e.activation(silu[:], bank[n][:, 0:I], ACT.Silu), [t, r.get("silu_read")])
            t = dve.add(lambda e: e.tensor_tensor(up[j % 2][:], silu[:], bank[n][:, I:SI], ALU.mult),
                        [t, r.get(("up_read", j - 2))])
            r["silu_read"] = r["up", j] = t
            free[n] = [t]

        def weights(j, m, first, n, rows):
            return wexp[0:rows, bass.ds(regs["w", j] + m * WE + first, n)]

        def fetch_weights(j):
            js = range(j, min(j + LOADS, NBLK))

            def build(e):
                for j_, reg in zip(js, load_registers(e, "offset", off_t[0:1, j:j + len(js)])):
                    regs["w", j_] = e.snap(reg, min_val=0, max_val=(E - 1) * 2 * WE)
            pe.add(build, [t_off], signal=False)

        def turn_hidden(j):
            n = (4, 5)[j % 2]
            for c in range(NC_E):
                t = pe.add(lambda e, c=c: e.transpose(bank[n][0:IC, c * P:(c + 1) * P],
                                                      up[j % 2][:, c * IC:(c + 1) * IC], ident[:]),
                           [r["up", j], *free[n]], signal=(c == NC_E - 1))
            r["up_read", j] = t
            hi, lo = split([u[:] for u in upT[j % 2]], bank[n][0:IC, 0:NC_E * P].rearrange("p (c t) -> p c t", c=NC_E),
                           [t, r.get(("upT_read", j - 2))])
            free[n] = [lo]
            r["upT", j] = lo

        def result(j):
            n = (6, 7)[j % 2]
            t = product(bank[n][:, 0:D], lambda s, k: upT[j % 2][s][:, k, :],
                        lambda m, k: weights(j, m, KT * SI + k * D, D, IC), NC_E,
                        [r["upT", j], *free[n]])
            r["upT_read", j] = t
            t = act.add(lambda e: e.activation(yb[j % NYB][:], bank[n][:, 0:D], ACT.Copy, scale=weight[j % NW][:]),
                        [t, r["weight", j], r.get(("add", j - NYB))])
            free[n] = [t]
            r["y", j] = t
            r["add", j] = pool.dma(lambda e: e.indirect_dma_start(
                acc_scr[j % NACC][:, :], bass.IndirectOffsetOnAxis(ap=token[j % NW][:].bitcast(U32), axis=0),
                yb[j % NYB][:], None, compute_op=ALU.add), d_add[j % NACC],
                [t, r.get(("add", j - NACC)), (d_zero.sem, d_zero.count), *((d.sem, d.count) for d in d_base)])

        for j in range(NXB - 1):
            load_rows(j)
        fetch_weights(0)
        for s in range(NBLK + 3):
            if s < NBLK:
                turn_rows(s)
            if s + NXB - 1 < NBLK:
                load_rows(s + NXB - 1)
            if 0 <= s - 1 < NBLK:
                hidden(s - 1)
            if 0 <= s - 2 < NBLK:
                turn_hidden(s - 2)
            if 0 <= s - 3 < NBLK:
                result(s - 3)

        part2.close()
        part3 = ExitStack()
        NF, TF = 4, 4
        acc = [[sb(f"acc{i}_{k}", [P, TF, D], F32, part3) for k in range(NACC)] for i in range(NF)]
        d_acc = [done(f"d_acc{i}") for i in range(NF)]
        d_out = [done(f"d_out{i}") for i in range(NF)]
        added = [(d.sem, d.count) for d in d_add] + [(u.sem, u.count) for u in (pe, act, dve, pool)]
        out_rows = out.rearrange("b s d -> (b s) d")
        for f in range(NT // TF):
            i = f % NF
            rows = slice(f * TF * P, (f + 1) * TF * P)
            for k in range(NACC):
                t = sp.dma(lambda e, i=i, k=k, rows=rows: e.dma_start(
                    acc[i][k][:], acc_scr[k][rows, :].rearrange("(p n) d -> p n d", n=TF)), d_acc[i],
                    [r.get(("out", f - NF)), *added])
            t = dve.add(lambda e, i=i: e.tensor_tensor(acc[i][0][:], acc[i][0][:], acc[i][1][:], ALU.add), [t])
            r["out", f] = act.dma(lambda e, i=i, rows=rows: e.dma_start(
                out_rows[rows, :].rearrange("(p n) d -> p n d", n=TF), acc[i][0][:]), d_out[i], [t])
        part3.close()

        finish(nc, ctx, (sp, act, dve, pool, pe), [d_scr, d_zero, *d_base, *d_rows, d_tail, *d_add, *d_out])


def finish(nc, ctx, queues, dones):
    sp, act, dve, pool, pe = queues
    with nc.Block() as block:
        @block.sync
        def _(eng):
            sp.emit(eng)
            for d in dones:
                if d.count:
                    eng.wait_ge(d.sem, d.count)

        @block.scalar
        def _(eng):
            act.emit(eng)

        @block.vector
        def _(eng):
            dve.emit(eng)

        @block.gpsimd
        def _(eng):
            pool.emit(eng)

        @block.tensor
        def _(eng):
            pe.emit(eng)


def kernel(L0_attn_x, L0_attn_Wqkv, L0_attn_Wo, L0_ffn_Wg, L0_ffn_W1, L0_ffn_W3, L0_ffn_W2, L0_ffn_Ws1, L0_ffn_Ws3,
           L0_ffn_Ws2):
    import numpy as np
    import concourse.bacc as bacc
    from concourse.bass_utils import run_bass_kernel_spmd

    inv = (1.0 / 10000.0 ** (2.0 * np.arange(PAIRS, dtype=np.float32) / HD)).astype(np.float32)
    angle = np.repeat(np.outer(inv, np.arange(S, dtype=np.float32)).astype(np.float32), H, axis=0)
    w = np.asarray(L0_attn_Wqkv)
    cols = np.arange(D).reshape(H, PAIRS, 2).transpose(2, 1, 0).reshape(-1)
    order = np.concatenate([cols, D + cols, np.arange(2 * D, 3 * D)])
    s1, s3 = np.asarray(L0_ffn_Ws1).T, np.asarray(L0_ffn_Ws3).T
    w1, w3, w2 = (np.asarray(v).transpose(0, 2, 1) for v in (L0_ffn_W1, L0_ffn_W3, L0_ffn_W2))
    wexp = np.zeros((E, P, WE), np.float32)
    wexp[:, :, :KT * SI] = (np.concatenate([w1, w3], axis=2).reshape(E, KT, P, SI).transpose(0, 2, 1, 3)
                            .reshape(E, P, KT * SI))
    wexp[:, :IC, KT * SI:] = w2.reshape(E, NC_E, IC, D).transpose(0, 2, 1, 3).reshape(E, IC, NC_E * D)
    arrays = {
        "x": np.ascontiguousarray(L0_attn_x),
        "wqkv": np.ascontiguousarray(w[:, order]),
        "wo": np.ascontiguousarray(L0_attn_Wo),
        "wsg": np.ascontiguousarray(np.concatenate([s1[:, :I], s3[:, :I], np.asarray(L0_ffn_Wg).T, s1[:, I:], s3[:, I:]],
                                                   axis=1)),
        "ws2": np.ascontiguousarray(np.asarray(L0_ffn_Ws2).T),
        "wexp": wexp,
        "rope_cos": np.cos(angle).astype(np.float32),
        "rope_sin": np.sin(angle).astype(np.float32),
    }
    nc = bacc.Bacc("TRN2", target_bir_lowering=False, num_devices=1)
    aps = {n: nc.dram_tensor(f"in_{n}", v.shape, mybir.dt.from_np(v.dtype), kind="ExternalInput").ap()
           for n, v in arrays.items()}
    out = nc.dram_tensor("out_0", (B, S, D), F32, kind="ExternalOutput").ap()
    layer_kernel(nc, aps, out)
    r = run_bass_kernel_spmd(nc, [{f"in_{n}": v for n, v in arrays.items()}], core_ids=[0])
    return r.results[0]["out_0"]
```
